# Optimizing a Trainium2 kernel written in Bass

```python
import numpy as np
import jax
import jax.numpy as jnp

def _softmax(x, axis=-1):
    return jax.nn.softmax(x, axis=axis)

def _gelu(x):
    return jax.nn.gelu(x, approximate=True)

def _silu(x):
    return jax.nn.silu(x)

def _sigmoid(x):
    return jax.nn.sigmoid(x)

def _layernorm(x, axis=-1, eps=1e-05):
    m = jnp.mean(x, axis=axis, keepdims=True)
    v = jnp.var(x, axis=axis, keepdims=True)
    return (x - m) / jnp.sqrt(v + eps)

def _scatter_add(tgt, idx, src, axis=0):
    return tgt.at[idx].add(src)

def _segment_sum(src, seg, n):
    return jax.ops.segment_sum(src, seg, n)
kernel_name = 'mk_recurrent_d1_jaxref_r8_a4db24'

def setup_inputs(seed: int=0):
    np.random.seed(seed)
    _w = jnp.asarray

    def _L0_attn_setup():
        import jax, jax.numpy as jnp
        import numpy as np
        MAX_WAVELENGTH = 10000.0
        NEG_INF = -1000000000.0

        def apply_rope(x):
            S, D = (x.shape[1], x.shape[-1])
            inv_freq = 1.0 / MAX_WAVELENGTH ** (jnp.arange(0, D, 2, dtype=jnp.float32) / D)
            t = jnp.arange(S, dtype=jnp.float32)[:, None] * inv_freq[None, :]
            emb = jnp.concatenate([t, t], axis=-1)
            cos = jnp.cos(emb)[None, :, None, :].astype(x.dtype)
            sin = jnp.sin(emb)[None, :, None, :].astype(x.dtype)
            x1, x2 = jnp.split(x, 2, axis=-1)
            rotated = jnp.concatenate([-x2, x1], axis=-1)
            return x * cos + rotated * sin
        key = jax.random.key(seed)
        k1, k2, k3 = jax.random.split(key, 3)
        B, S, dim = (2, 256, 128)
        x = jax.random.normal(k1, (B, S, dim), dtype=jnp.float32)
        w_qkv = jax.random.normal(k2, (dim, 3 * dim), dtype=jnp.float32) * dim ** (-0.5)
        w_proj = jax.random.normal(k3, (dim, dim), dtype=jnp.float32) * dim ** (-0.5)
        b_proj = jnp.zeros((dim,), dtype=jnp.float32)
        return {'x': x, 'w_qkv': w_qkv, 'w_proj': w_proj, 'b_proj': b_proj}
    _L0_attn_in = _L0_attn_setup()

    def _L0_ffn_setup():
        import jax, jax.numpy as jnp
        import numpy as np
        DIM = 128
        HIDDEN = 384
        SCALE = 1.0 / 127.0

        def _dequant(w_int, dtype):
            return w_int.astype(dtype) * jnp.asarray(SCALE, dtype)
        key = jax.random.key(seed)
        k_x, k_g, k_u, k_d = jax.random.split(key, 4)
        x = jax.random.normal(k_x, (4, 256, DIM), dtype=jnp.float32)
        w_gate = jax.random.randint(k_g, (HIDDEN, DIM), -127, 128, dtype=jnp.int32)
        w_up = jax.random.randint(k_u, (HIDDEN, DIM), -127, 128, dtype=jnp.int32)
        w_down = jax.random.randint(k_d, (DIM, HIDDEN), -127, 128, dtype=jnp.int32)
        return {'x': x, 'w_gate': w_gate, 'w_up': w_up, 'w_down': w_down}
    _L0_ffn_in = _L0_ffn_setup()
    _d = {'L0_attn_x': _L0_attn_in['x'], 'L0_attn_w_qkv': _L0_attn_in['w_qkv'], 'L0_attn_w_proj': _L0_attn_in['w_proj'], 'L0_attn_b_proj': _L0_attn_in['b_proj'], 'L0_ffn_w_gate': _L0_ffn_in['w_gate'], 'L0_ffn_w_up': _L0_ffn_in['w_up'], 'L0_ffn_w_down': _L0_ffn_in['w_down']}
    _x0 = _d['L0_attn_x']
    _d['L0_attn_x'] = jax.random.normal(jax.random.fold_in(jax.random.key(seed), 1), (8, 512, 128), dtype=_x0.dtype)
    del _x0
    return _d

def reference(L0_attn_x, L0_attn_w_qkv, L0_attn_w_proj, L0_attn_b_proj, L0_ffn_w_gate, L0_ffn_w_up, L0_ffn_w_down):

    def _L0_attn_ref(x, w_qkv, w_proj, b_proj):
        import jax, jax.numpy as jnp
        import numpy as np
        MAX_WAVELENGTH = 10000.0
        NEG_INF = -1000000000.0

        def apply_rope(x):
            S, D = (x.shape[1], x.shape[-1])
            inv_freq = 1.0 / MAX_WAVELENGTH ** (jnp.arange(0, D, 2, dtype=jnp.float32) / D)
            t = jnp.arange(S, dtype=jnp.float32)[:, None] * inv_freq[None, :]
            emb = jnp.concatenate([t, t], axis=-1)
            cos = jnp.cos(emb)[None, :, None, :].astype(x.dtype)
            sin = jnp.sin(emb)[None, :, None, :].astype(x.dtype)
            x1, x2 = jnp.split(x, 2, axis=-1)
            rotated = jnp.concatenate([-x2, x1], axis=-1)
            return x * cos + rotated * sin
        B, S, dim = x.shape
        heads = 16
        head_dim = dim // heads
        scale = head_dim ** (-0.5)
        qkv = x @ w_qkv
        qkv = qkv.reshape(B, S, 3, heads, head_dim)
        Q, K, V = (qkv[:, :, 0], qkv[:, :, 1], qkv[:, :, 2])
        Q = apply_rope(Q)
        K = apply_rope(K)
        attn = jnp.einsum('bqhd,bkhd->bhqk', Q, K) * scale
        causal = jnp.tril(jnp.ones((S, S), dtype=bool))[None, None]
        attn = jnp.where(causal, attn, jnp.asarray(NEG_INF, attn.dtype))
        attn = jax.nn.softmax(attn, axis=-1)
        out = jnp.einsum('bhqk,bkhd->bqhd', attn, V).reshape(B, S, dim)
        return out @ w_proj + b_proj

    def _L0_ffn_ref(x, w_gate, w_up, w_down):
        import jax, jax.numpy as jnp
        import numpy as np
        DIM = 128
        HIDDEN = 384
        SCALE = 1.0 / 127.0

        def _dequant(w_int, dtype):
            return w_int.astype(dtype) * jnp.asarray(SCALE, dtype)
        wg = _dequant(w_gate, x.dtype)
        wu = _dequant(w_up, x.dtype)
        wd = _dequant(w_down, x.dtype)
        gate = jnp.einsum('bsd,hd->bsh', x, wg)
        up = jnp.einsum('bsd,hd->bsh', x, wu)
        h = jax.nn.silu(gate) * up
        return jnp.einsum('bsh,dh->bsd', h, wd)
    x = L0_attn_x
    xn = _layernorm(x, axis=-1)
    s = _L0_attn_ref(xn, L0_attn_w_qkv, L0_attn_w_proj, L0_attn_b_proj)
    g = _silu(_L0_ffn_ref(xn, L0_ffn_w_gate, L0_ffn_w_up, L0_ffn_w_down))
    x = x + s * g
    return x

_drawn_inputs = setup_inputs


def setup_inputs(seed=0):
    import zlib

    import numpy as np

    out = dict(_drawn_inputs(seed))
    spreads = {'L0_attn_b_proj': (0.0, 0.1)}
    factors = {}
    for name, (base, spread) in spreads.items():
        noise = np.random.default_rng([zlib.crc32(name.encode()), seed]).standard_normal(out[name].shape)
        drawn = base * np.exp(spread * noise) if base else spread * noise
        out[name] = jnp.asarray(drawn.astype(out[name].dtype))
    for name, factor in factors.items():
        out[name] = (out[name] * factor).astype(out[name].dtype)
    return out
```

```python
import concourse.bass as bass
from concourse import mybir
from contextlib import ExitStack

B, S, D = 8, 512, 128
H, DH = 16, 8
HID = 384
P = 128
TB = S // P
NT = B * TB
HC = HID // P
GH = 4
NG = H // GH
GROUPS = B * NG
NPROD = 6
ROWS = NPROD * DH
SHIFT_ROW = 96
PAIRS = ("hml", "hm", "h")
TILES = 10
ER, MR = 4, 2
EPS = 1e-5
MASKED = -1.0e9


def wait(eng, sem, value):
    if isinstance(value, int) and value <= 0:
        return
    eng.wait_ge(sem, value)


def wait_apart(eng, sem, value, met, met_value):
    if not isinstance(value, int):
        value = eng.to_reg(value)
    eng.wait_ge(met, met_value)
    wait(eng, sem, value)


def exists(b, g):
    return not isinstance(b, int) or 0 <= NG * b + g < GROUPS


def attn_ffn_block(nc, x, w_qkv, w_proj, b_proj, w_gate, w_up, w_down,
                   cos_t, sin_t, ident_f, ident_h, mask_h, scratch, out):
    fp32 = mybir.dt.float32
    bf16 = mybir.dt.bfloat16
    i32 = mybir.dt.int32
    ALU = mybir.AluOpType
    ACT = mybir.ActivationFunctionType
    AX = mybir.AxisListType
    SCALE = float(DH) ** -0.5

    x_v = x.rearrange("b (t p) d -> p (b t) d", p=P)
    out_v = out.rearrange("b (t p) d -> p (b t) d", p=P)

    ctx = ExitStack()
    with ctx:
        def sb(name, shape, dt=fp32):
            return ctx.enter_context(nc.sbuf_tensor(name, shape, dt))

        def sem(name):
            return ctx.enter_context(nc.semaphore(name))

        cosT, sinT = sb("cosT", [P, S]), sb("sinT", [P, S])
        idf, idh = sb("idf", [P, P]), sb("idh", [P, P], bf16)
        maskh = sb("maskh", [P, P], bf16)
        wqkv, wqk = sb("wqkv", [P, 3 * D]), sb("wqk", [P, 2, D])
        wp, bias = sb("wp", [P, D]), sb("bias", [P, D])
        wgT, wuT, wdT = sb("wgT", [P, HC, P]), sb("wuT", [P, HC, P]), sb("wdT", [P, HC, P])
        x_all = sb("x_all", [P, NT, D])
        gate_all = sb("gate_all", [P, NT, D])
        v_all = sb("v_all", [P, NT, D])
        stats, t6 = sb("stats", [P, NT, 6]), sb("t6", [P, 4, NT])
        mean, rstd = sb("mean", [P, NT]), sb("rstd", [P, NT])
        xnT = sb("xnT", [P, S])
        thf = sb("thf", [P, S])
        th, ups, t1 = sb("th", [P, HC, S]), sb("ups", [P, HC, S]), sb("t1", [P, HC, S])
        hT = sb("hT", [P, HC, S])
        ropc, rops, roped, rest = (sb("ropc", [P, 2, S]), sb("rops", [P, 2, S]),
                                   sb("roped", [P, 2, S]), sb("rest", [P, 2, S]))
        parts = sb("parts", [P, 2, 3, S], bf16)
        QA, KA = sb("QA", [P, NG, GH, S], bf16), sb("KA", [P, NG, GH, S], bf16)
        PT = sb("PT", [P, 2, GH, 1280])
        Vb = sb("Vb", [P, TB, 2, GH, 2, 32])
        rmax, nmax = sb("rmax", [P, GH, TB]), sb("nmax", [P, 3, GH * TB])
        msp, mT = sb("msp", [P, 8, GH * TB], bf16), sb("mT", [3 * GH * TB, 2, P], bf16)
        OS, rl, AN, AT = sb("OS", [P, S]), sb("rl", [P, TB, 8]), sb("AN", [P, TB, D]), sb("AT", [P, S])
        sS, fo = sb("sS", [P, TB, D]), sb("fo", [P, TB, D])
        pt_flat = PT[:, :, :, :].rearrange("p a h c -> p (a h c)")
        xn = pt_flat[:, 0:S].rearrange("p (t d) -> p t d", d=D)
        wi = pt_flat[:, S:S + 3 * HID].bitcast(i32).rearrange("p (w c k) -> p w c k", w=3, c=HC)
        wf = pt_flat[:, S + 3 * HID:S + 6 * HID].rearrange("p (w c k) -> p w c k", w=3, c=HC)

        bank = [ctx.enter_context(nc.psum_tensor(f"bank{i}", [P, S], fp32)) for i in range(8)]

        consts_in, wi_in, x_in = sem("consts_in"), sem("wi_in"), [sem(f"x_in{i}") for i in range(4)]
        dve_prep, pool_prep = sem("dve_prep"), sem("pool_prep")
        var_ready, std_ready, xn_ready = sem("var_ready"), sem("std_ready"), sem("xn_ready")
        wf_ready, wT_done, wT_ready = sem("wf_ready"), sem("wT_done"), sem("wT_ready")
        tp_done, xnT_ready = sem("tp_done"), sem("xnT_ready")
        gate_done, up_done, th_ready, up_copied, t1_ready, h_ready = (
            sem("gate_done"), sem("up_done"), sem("th_ready"), sem("up_copied"), sem("t1_ready"), sem("h_ready"))
        down_done, thf_ready, g_stored = sem("down_done"), sem("thf_ready"), sem("g_stored")
        q_done, k_done, v_done, v_stored = sem("q_done"), sem("k_done"), sem("v_done"), sem("v_stored")
        q_roped, k_roped, roped_ready = sem("q_roped"), sem("k_roped"), sem("roped_ready")
        hi_ready, rest_ready, mid_ready, lo_ready = (
            sem("hi_ready"), sem("rest_ready"), sem("mid_ready"), sem("lo_ready"))
        parts_written = sem("parts_written")
        aug_in = [sem(f"aug_in{i}") for i in range(NG)]
        shift_in = [sem("shift_in0"), sem("shift_in1")]
        e_done, exp_done, m_done, red_done = sem("e_done"), sem("exp_done"), sem("m_done"), sem("red_done")
        masked, pv_done, o_copied, vb_ready = sem("masked"), sem("pv_done"), sem("o_copied"), sem("vb_ready")
        rmax_chain, msp_ready, mt_done, mt_copied = (
            sem("rmax_chain"), sem("msp_ready"), sem("mt_done"), sem("mt_copied"))
        tr_done, rl_ready, norm_ready, ant_done, at_copied = (
            sem("tr_done"), sem("rl_ready"), sem("norm_ready"), sem("ant_done"), sem("at_copied"))
        proj_done, s_ready, sg_ready, f_ready, out_written = (
            sem("proj_done"), sem("s_ready"), sem("sg_ready"), sem("f_ready"), sem("out_written"))

        block = ctx.enter_context(nc.Block())

        def exp_blocks(k):
            if k < 4:
                return [(0, k, 0)]
            if k < 8:
                return [(0, k - 4, 1), (384, k - 4, 3)]
            return [(0, 2 * (k - 8), 2), (256, 2 * (k - 8) + 1, 2)]

        def max_blocks(k):
            pair, r = divmod(k, 5)
            if r < 2:
                return [(0, 2 * pair + r, 3)]
            if r < 4:
                return [(0, 2 * pair + r - 2, 2), (384, 2 * pair + r - 2, 0)]
            return [(0, 2 * pair, 1), (256, 2 * pair + 1, 1)]

        KEY_COL = {0: 0, 1: 512, 3: 896, 2: 1024}

        def attention_steps(eng, step):
            for g in (2, 3):
                step(-1, g)
            for g in range(2 * NG):
                step(g // NG, g % NG)
            with eng.Fori(2, B - 1) as b:
                for g in range(NG):
                    step(b, g)
            for g in range(NG):
                step(B - 1, g)
            for g in range(3):
                step(B, g)

        @block.sync
        def _(sp):
            for i in range(4):
                sp.dma_start(x_all[:, 8 * i:8 * i + 8, :], x_v[:, 8 * i:8 * i + 8, :]).then_inc(x_in[i], 16)
            sp.dma_start(wi[:, 0, :, :], w_gate.rearrange("(c p) k -> p c k", p=P)).then_inc(wi_in, 16)
            sp.dma_start(wi[:, 1, :, :], w_up.rearrange("(c p) k -> p c k", p=P)).then_inc(wi_in, 16)
            sp.dma_start(wi[:, 2, :, :], w_down.rearrange("p (c k) -> p c k", c=HC)).then_inc(wi_in, 16)

            def write_parts(b):
                wait_apart(sp, lo_ready, b + 1, wi_in, 48)
                row = 0
                for n, names in enumerate(PAIRS):
                    m = len(names)
                    dst_q = scratch[b, 0, row:row + m * DH].rearrange("(a d) h t -> (d h) a t", a=m)
                    dst_k = scratch[b, 1, row:row + m * DH].rearrange("(a d) h t -> (d h) a t", a=m)
                    sp.dma_start(dst_q, parts[:, 0, 0:m, :]).then_inc(parts_written, 16)
                    sp.dma_start(dst_k, parts[:, 1, n:n + 1, :].broadcast_to([P, m, S])).then_inc(parts_written, 16)
                    row += m * DH

            with sp.Fori(0, B) as b:
                write_parts(b)

            def load_aug(b, g):
                if not exists(b, g):
                    return
                bb, slot = b + g // NG, g % NG
                first = (slot // 2) * 8 + slot % 2
                wait_apart(sp, e_done, b * (TILES * NG) + TILES * (g - NG + 1), wi_in, 48)
                for side, dst in ((0, QA), (1, KA)):
                    sp.dma_start(dst[0:ROWS, slot, :, :],
                                 scratch[bb, side, :, first:first + 7:2, :]).then_inc(aug_in[slot], 16)

            def step(b, g):
                load_aug(b, g + 3)
                if exists(b, g + 1):
                    gn = g + 1
                    wait_apart(sp, mt_copied, b * NG + gn + 1, wi_in, 48)
                    wait_apart(sp, e_done, b * (TILES * NG) + TILES * (gn - NG + 1), wi_in, 48)
                    for part in range(3):
                        sp.dma_start(QA[SHIFT_ROW + part:SHIFT_ROW + part + 1, gn % NG, :, :].rearrange("o h (i q) -> o (h i) q", q=P),
                                     mT[16 * part:16 * part + 16, gn % 2, :]).then_inc(shift_in[gn % 2], 16)
                if g == 3 and exists(b, 0) and (not isinstance(b, int) or b >= 1):
                    store(b - 1)

            def store(b):
                wait_apart(sp, f_ready, b + 1, wi_in, 48)
                sp.dma_start(out_v[:, bass.ds(b * TB, TB), :], fo[:, :, :]).then_inc(out_written, 16)

            wait(sp, parts_written, 16 * 6 * B)
            wait(sp, pool_prep, 7)
            load_aug(-1, 4)
            attention_steps(sp, step)
            store(B - 1)
            wait(sp, out_written, 16 * B)

        @block.gpsimd
        def _(pool):
            nc.gpsimd.memset(QA[:, :, :, :], 0.0).then_inc(pool_prep, 1)
            nc.gpsimd.memset(KA[:, :, :, :], 0.0).then_inc(pool_prep, 1)
            pool.wait_ge(pool_prep, 2)
            nc.gpsimd.memset(KA[SHIFT_ROW:SHIFT_ROW + 3, :, :, :], 1.0).then_inc(pool_prep, 1)
            pool.wait_ge(pool_prep, 3)
            nc.gpsimd.memset(Vb[:, :, :, :, :, :], 0.0).then_inc(pool_prep, 1)
            pool.wait_ge(pool_prep, 4)
            nc.gpsimd.memset(msp[:, 3:8, :], 0.0).then_inc(pool_prep, 1)
            for gl in range(2):
                nc.gpsimd.memset(Vb[:, :, :, :, gl, 16 * gl + DH:16 * gl + 2 * DH], 1.0).then_inc(pool_prep, 1)

            def hidden(b):
                for c in range(HC):
                    wait(pool, t1_ready, b * HC + c + 1)
                    wait(pool, up_copied, b * HC + c + 1)
                    if c == 0:
                        wait(pool, down_done, b)
                    nc.gpsimd.tensor_tensor(hT[:, c, :], t1[:, c, :], ups[:, c, :], ALU.mult).then_inc(h_ready, 1)

            def low_parts(b):
                wait(pool, mid_ready, b + 1)
                nc.gpsimd.tensor_tensor(parts[:, :, 2, :], rest[:, :, :], parts[:, :, 1, :],
                                        ALU.subtract).then_inc(lo_ready, 1)

            hidden(0)
            hidden(1)
            low_parts(0)
            with pool.Fori(2, B) as b:
                hidden(b)
                low_parts(b - 1)
            low_parts(B - 1)

            def step(b, g):
                if g % 2 == 0 and exists(b, g):
                    half = g // 2
                    wait(pool, pv_done, b * (4 * NG) + 4 * (g - 2))
                    wait(pool, v_stored, B)
                    wait(pool, pool_prep, 7)
                    for gl in range(2):
                        src = v_all[:, bass.ds(b * TB, TB), :].rearrange(
                            "p t (f c a d) -> p t f c a d", f=2, c=GH, a=2)[:, :, half, :, gl, :]
                        nc.gpsimd.tensor_copy(Vb[:, :, half, :, gl, 16 * gl:16 * gl + DH], src).then_inc(vb_ready, 1)
                if exists(b, g):
                    par = g % 2
                    for j, after in ((0, 4), (1, 8), (3, 8), (2, 10)):
                        wait_apart(pool, exp_done, b * (TILES * NG) + TILES * g + after, pool_prep, 7)
                        blk = PT[:, par, :, KEY_COL[j]:KEY_COL[j] + P]
                        nc.gpsimd.affine_select(out=blk, in_=blk, compare_op=ALU.is_ge, fill=0.0, base=0,
                                                pattern=[[0, GH], [1, P]],
                                                channel_multiplier=-1).then_inc(masked, 1)
                if g == 3 and (not isinstance(b, int) or 1 <= b < B):
                    finish(b - 1)

            def finish(b):
                wait(pool, s_ready, b + 1)
                wait(pool, out_written, b * 16)
                nc.gpsimd.tensor_tensor(sS[:, :, :], sS[:, :, :], gate_all[:, bass.ds(b * TB, TB), :],
                                        ALU.mult).then_inc(sg_ready, 1)
                wait(pool, sg_ready, b + 1)
                nc.gpsimd.tensor_tensor(fo[:, :, :], sS[:, :, :], x_all[:, bass.ds(b * TB, TB), :],
                                        ALU.add).then_inc(f_ready, 1)

            wait(pool, g_stored, B)
            attention_steps(pool, step)
            finish(B - 1)

        @block.scalar
        def _(act):
            for dst, src in ((idf[:, :], ident_f), (wqkv[:, :], w_qkv), (wp[:, :], w_proj),
                             (bias[:, :], b_proj.rearrange("(o d) -> o d", o=1).broadcast_to([P, D])),
                             (cosT[:, :], cos_t), (sinT[:, :], sin_t), (idh[:, :], ident_h),
                             (maskh[:, :], mask_h)):
                act.dma_start(dst, src).then_inc(consts_in, 16)
            act.wait_ge(var_ready, 1)
            nc.scalar.activation(rstd[:, :], rstd[:, :], ACT.Sqrt).then_inc(std_ready, 1)
            for w, dst in enumerate((wgT, wuT, wdT)):
                act.wait_ge(wT_done, w + 1)
                nc.scalar.activation(dst[:, :, :].rearrange("p c k -> p (c k)"), bank[2 + w][:, 0:HID],
                                     ACT.Copy, scale=0.5 if w == 2 else 1.0).then_inc(wT_ready, 1)

            def normed(b):
                wait(act, tp_done, b + 1)
                wait(act, v_done, b)
                nc.scalar.activation(xnT[:, :], bank[0][:, :], ACT.Copy).then_inc(xnT_ready, 1)

            def outer_tanh(b):
                wait(act, down_done, b + 1)
                wait(act, g_stored, b)
                nc.scalar.activation(thf[:, :], bank[1][:, :], ACT.Tanh, scale=0.5).then_inc(thf_ready, 1)

            def chunk(b, c):
                wait(act, gate_done, b * HC + c + 1)
                wait(act, t1_ready, (b - 1) * HC + c + 1)
                nc.scalar.activation(th[:, c, :], bank[2 + 2 * c][:, :], ACT.Tanh, scale=0.5).then_inc(th_ready, 1)
                wait(act, up_done, b * HC + c + 1)
                wait(act, h_ready, (b - 1) * HC + c + 1)
                nc.scalar.activation(ups[:, c, :], bank[3 + 2 * c][:, :], ACT.Copy).then_inc(up_copied, 1)

            def high_parts(b):
                wait(act, roped_ready, b + 1)
                wait(act, parts_written, b * 96)
                nc.scalar.activation(parts[:, :, 0, :], roped[:, :, :], ACT.Copy).then_inc(hi_ready, 1)

            def mid_parts(b):
                wait(act, rest_ready, b + 1)
                nc.scalar.activation(parts[:, :, 1, :], rest[:, :, :], ACT.Copy).then_inc(mid_ready, 1)

            def store_v(b):
                wait(act, v_done, b + 1)
                nc.scalar.activation(v_all[:, bass.ds(b * TB, TB), :].rearrange("p t d -> p (t d)"),
                                     bank[4][:, :], ACT.Copy).then_inc(v_stored, 1)

            def batch(b, first):
                normed(b)
                if not first:
                    outer_tanh(b - 1)
                chunk(b, 0)
                if not first:
                    high_parts(b - 1)
                chunk(b, 1)
                if not first:
                    mid_parts(b - 1)
                chunk(b, 2)
                store_v(b)

            batch(0, True)
            batch(1, False)
            with act.Fori(2, B) as b:
                batch(b, False)
            outer_tanh(B - 1)
            high_parts(B - 1)
            mid_parts(B - 1)

            def copy_o(b, half):
                wait(act, pv_done, b * (4 * NG) + 8 * half + 8)
                wait(act, tr_done, b * 2 + half)
                nc.scalar.activation(OS[:, :], bank[6][:, :], ACT.Copy).then_inc(o_copied, 1)

            def step(b, g):
                for k in range(TILES):
                    if exists(b, g):
                        n = b * (TILES * NG) + TILES * g + k
                        wait(act, e_done, n + 1)
                        if k == 0:
                            wait(act, pv_done, b * (4 * NG) + 4 * (g - 1))
                        src = bank[(TILES * g + k) % ER][:, :]
                        if k < 4:
                            dst = PT[:, g % 2, k, 0:512]
                        elif k < 8:
                            dst = PT[:, g % 2, k - 4, 512:1024]
                        else:
                            dst = PT[:, g % 2, 2 * (k - 8):2 * (k - 8) + 2, 1024:1280]
                            src = src.rearrange("p (h q) -> p h q", h=2)
                        nc.scalar.activation(dst, src, ACT.Exp, scale=SCALE).then_inc(exp_done, 1)
                    if k == 7 and g == 2 and (not isinstance(b, int) or b >= 1):
                        wait(act, ant_done, b)
                        wait(act, proj_done, b - 1)
                        nc.scalar.activation(AT[:, :], bank[7][:, :], ACT.Copy).then_inc(at_copied, 1)
                if g == 0 and (not isinstance(b, int) or b >= 1):
                    copy_o(b - 1, 1)
                if g == 2 and exists(b, g) and (not isinstance(b, int) or b >= 0):
                    copy_o(b, 0)

            attention_steps(act, step)

        @block.vector
        def _(dve):
            for i in range(4):
                dve.wait_ge(x_in[i], 16)
                with dve.Fori(2 * i, 2 * i + 2) as b:
                    for u in range(TB):
                        nc.vector.bn_stats(stats[:, b * TB + u, :], x_all[:, b * TB + u, :]).then_inc(dve_prep, 1)
            dve.wait_ge(dve_prep, NT)
            n = [NT]

            def link(ins):
                n[0] += 1
                ins.then_inc(dve_prep, 1)
                dve.wait_ge(dve_prep, n[0])

            me, se, mo, so = (stats[:, :, i] for i in (1, 2, 4, 5))
            link(nc.vector.tensor_tensor(t6[:, 0, :], me, mo, ALU.add))
            link(nc.vector.tensor_tensor(t6[:, 1, :], me, mo, ALU.subtract))
            link(nc.vector.tensor_tensor(t6[:, 2, :], se, so, ALU.add))
            link(nc.vector.tensor_scalar(mean[:, :], t6[:, 0, :], 0.5, None, ALU.mult))
            link(nc.vector.tensor_tensor(t6[:, 3, :], t6[:, 1, :], t6[:, 1, :], ALU.mult))
            link(nc.vector.tensor_scalar(t6[:, 2, :], t6[:, 2, :], 1.0 / D, EPS, ALU.mult, ALU.add))
            nc.vector.scalar_tensor_tensor(out=rstd[:, :], in0=t6[:, 3, :], scalar=0.25, in1=t6[:, 2, :],
                                           op0=ALU.mult, op1=ALU.add).then_inc(var_ready, 1)
            dve.wait_ge(wi_in, 48)
            for w in range(3):
                nc.vector.tensor_scalar(wf[:, w, :, :], wi[:, w, :, :], 1.0 / 127.0, None,
                                        ALU.mult).then_inc(wf_ready, 1)
            dve.wait_ge(consts_in, 8 * 16)
            for i in range(2):
                nc.vector.tensor_copy(wqk[:, i, :].rearrange("p (d h) -> p d h", d=DH),
                                      wqkv[:, i * D:(i + 1) * D].rearrange("p (h d) -> p d h", d=DH)
                                      ).then_inc(wf_ready, 1)
            link(nc.vector.tensor_scalar(wp[:, :], wp[:, :], 0.5, None, ALU.mult))
            link(nc.vector.tensor_scalar(bias[:, :], bias[:, :], 0.5, None, ALU.mult))
            dve.wait_ge(std_ready, 1)
            link(nc.vector.reciprocal(rstd[:, :], rstd[:, :]))

            def normalise_in(b):
                wait(dve, tp_done, b)
                for u in range(TB):
                    last = nc.vector.tensor_scalar(xn[:, u, :], x_all[:, b * TB + u, :],
                                                   mean[:, bass.ds(b * TB + u, 1)],
                                                   rstd[:, bass.ds(b * TB + u, 1)], ALU.subtract, ALU.mult)
                last.then_inc(xn_ready, 1)

            def outer_gate(b):
                wait(dve, thf_ready, b + 1)
                nc.vector.scalar_tensor_tensor(out=gate_all[:, bass.ds(b * TB, TB), :].rearrange("p t d -> p (t d)"),
                                               in0=thf[:, :], scalar=1.0, in1=bank[1][:, :],
                                               op0=ALU.add, op1=ALU.mult).then_inc(g_stored, 1)

            def gate(b, c):
                wait(dve, th_ready, b * HC + c + 1)
                wait(dve, h_ready, (b - 1) * HC + c + 1)
                nc.vector.scalar_tensor_tensor(out=t1[:, c, :], in0=th[:, c, :], scalar=1.0, in1=bank[2 + 2 * c][:, :],
                                               op0=ALU.add, op1=ALU.mult).then_inc(t1_ready, 1)

            def rest_of(b):
                wait(dve, hi_ready, b + 1)
                wait(dve, lo_ready, b)
                nc.vector.tensor_tensor(rest[:, :, :], roped[:, :, :], parts[:, :, 0, :],
                                        ALU.subtract).then_inc(rest_ready, 1)

            def rope(b):
                for i, (done, roped_sem) in enumerate(((q_done, q_roped), (k_done, k_roped))):
                    wait(dve, done, b + 1)
                    if i == 0:
                        wait(dve, roped_ready, b)
                    nc.vector.tensor_tensor(ropc[:, i, :], bank[2 + i][:, :], cosT[:, :],
                                            ALU.mult).then_inc(roped_sem, 1)
                    nc.vector.tensor_tensor(rops[0:64, i, :], bank[2 + i][64:128, :], sinT[64:128, :],
                                            ALU.mult).then_inc(roped_sem, 1)
                    nc.vector.tensor_tensor(rops[64:128, i, :], bank[2 + i][0:64, :], sinT[0:64, :],
                                            ALU.mult).then_inc(roped_sem, 1)
                wait(dve, q_roped, b * 3 + 3)
                wait(dve, k_roped, b * 3 + 3)
                wait(dve, rest_ready, b)
                nc.vector.tensor_tensor(roped[:, :, :], ropc[:, :, :], rops[:, :, :],
                                        ALU.add).then_inc(roped_ready, 1)

            def batch(b, first, last=False):
                if not first:
                    outer_gate(b - 1)
                if not last:
                    normalise_in(b + 1)
                gate(b, 0)
                if not first:
                    rest_of(b - 1)
                gate(b, 1)
                gate(b, 2)
                rope(b)

            normalise_in(0)
            batch(0, True)
            batch(1, False)
            with dve.Fori(2, B - 1) as b:
                batch(b, False)
            batch(B - 1, False, True)
            outer_gate(B - 1)
            rest_of(B - 1)

            def copy_shift(b, g):
                wait(dve, mt_done, b * NG + g + 1)
                wait(dve, shift_in[g % 2], b * 96 + 48 * ((g - 2) // 2 + 1))
                nc.vector.tensor_copy(mT[:, g % 2, :], bank[7][0:3 * GH * TB, 0:P // 2].bitcast(bf16)
                                      ).then_inc(mt_copied, 1)

            def normalise(b, half):
                wait(dve, tr_done, b * 2 + half + 1)
                v = bank[7][:, :].rearrange("p (t e w) -> p t e w", t=TB, w=2 * DH)
                nc.vector.reciprocal(rl[:, :, :], v[:, :, :, DH]).then_inc(rl_ready, 1)
                wait(dve, rl_ready, b * 2 + half + 1)
                wait(dve, ant_done, b)
                nc.vector.tensor_tensor(AN[:, :, 64 * half:64 * half + 64].rearrange("p t (e d) -> p t e d", d=DH),
                                        v[:, :, :, 0:DH],
                                        rl[:, :, :].rearrange("p t (e o) -> p t e o", o=1).broadcast_to([P, TB, 8, DH]),
                                        ALU.mult).then_inc(norm_ready, 1)

            def projected(b):
                wait(dve, proj_done, b + 1)
                wait(dve, f_ready, b)
                nc.vector.tensor_tensor(sS[:, :, :], bank[7][:, :].rearrange("p (t d) -> p t d", t=TB),
                                        bias[:, :].rearrange("p (o d) -> p o d", o=1).broadcast_to([P, TB, D]),
                                        ALU.add).then_inc(s_ready, 1)

            def step(b, g):
                later = not isinstance(b, int)
                for k in range(TILES):
                    if exists(b, g + 2):
                        n = b * (TILES * NG) + TILES * (g + 2) + k
                        wait(dve, m_done, n + 1)
                        if k == 0:
                            wait(dve, msp_ready, b * NG + g + 2)
                        src = bank[4 + k % MR]
                        blocks = max_blocks(k)
                        if blocks[0][2] == 1:
                            last = nc.vector.tensor_reduce(rmax[:, blocks[0][1]:blocks[0][1] + 2, 1],
                                                           src[:, :].rearrange("p (h q) -> p h q", h=2), AX.X, ALU.max)
                        else:
                            for col, h, i in blocks:
                                last = nc.vector.tensor_reduce(rmax[:, h, i:i + 1], src[:, col:col + P * (i + 1)],
                                                               AX.X, ALU.max)
                        last.then_inc(red_done, 1)
                    if k == 2 and exists(b, g + 1):
                        copy_shift(b, g + 1)
                    if k == 5 and g == 1 and (later or b >= 1):
                        normalise(b - 1, 1)
                    if k == 5 and g == 3 and exists(b, g):
                        normalise(b, 0)
                    if k == 8 and g == 2 and (later or b >= 1):
                        projected(b - 1)
                if exists(b, g + 2):
                    c = b * (5 * NG) + 5 * (g + 2)
                    wait(dve, red_done, b * (TILES * NG) + TILES * (g + 3))
                    wait(dve, mt_done, b * NG + g + 2)
                    flat = rmax[:, :, :].rearrange("p h i -> p (h i)")
                    for stage in range(5):
                        if stage == 0:
                            ins = nc.vector.tensor_scalar(nmax[:, 0, :], flat, -1.0, None, ALU.mult)
                        elif stage == 1:
                            ins = nc.vector.tensor_copy(msp[:, 0, :], nmax[:, 0, :])
                        elif stage == 2:
                            ins = nc.vector.tensor_tensor(nmax[:, 1, :], nmax[:, 0, :], msp[:, 0, :], ALU.subtract)
                        elif stage == 3:
                            ins = nc.vector.tensor_copy(msp[:, 1, :], nmax[:, 1, :])
                        else:
                            ins = nc.vector.tensor_tensor(msp[:, 2, :], nmax[:, 1, :], msp[:, 1, :], ALU.subtract)
                        if stage < 4:
                            ins.then_inc(rmax_chain, 1)
                            wait(dve, rmax_chain, b * (4 * NG) + 4 * (g + 2) + stage + 1)
                        else:
                            ins.then_inc(msp_ready, 1)

            attention_steps(dve, step)

        @block.tensor
        def _(pe):
            pe.wait_ge(consts_in, 8 * 16)
            pe.wait_ge(wf_ready, 3)
            for w in range(3):
                for c in range(HC):
                    last = nc.tensor.transpose(bank[2 + w][:, c * P:(c + 1) * P], wf[:, w, c, :], idf[:, :])
                last.then_inc(wT_done, 1)
            pe.wait_ge(wT_ready, 3)
            pe.wait_ge(wf_ready, 5)

            def transpose_in(b):
                wait(pe, xn_ready, b + 1)
                wait(pe, xnT_ready, b)
                for u in range(TB):
                    last = nc.tensor.transpose(bank[0][:, u * P:(u + 1) * P], xn[:, u, :], idf[:, :])
                last.then_inc(tp_done, 1)

            def down(b):
                wait(pe, h_ready, (b + 1) * HC)
                wait(pe, g_stored, b)
                for u in range(TB):
                    for c in range(HC):
                        last = nc.tensor.matmul(bank[1][:, u * P:(u + 1) * P], hT[:, c, u * P:(u + 1) * P],
                                                wdT[:, c, :], start=(c == 0), stop=(c == HC - 1))
                last.then_inc(down_done, 1)

            def products(b):
                wait(pe, xnT_ready, b + 1)
                free_gate = ((q_roped, b * 3), (v_stored, b), (t1_ready, b * HC))
                free_up = ((k_roped, b * 3), (up_copied, (b - 1) * HC + 2), (up_copied, b * HC))
                for c in range(HC):
                    wait(pe, *free_gate[c])
                    nc.tensor.matmul(bank[2 + 2 * c][:, :], wgT[:, c, :], xnT[:, :], start=True,
                                     stop=True).then_inc(gate_done, 1)
                    wait(pe, *free_up[c])
                    nc.tensor.matmul(bank[3 + 2 * c][:, :], wuT[:, c, :], xnT[:, :], start=True,
                                     stop=True).then_inc(up_done, 1)
                wait(pe, t1_ready, b * HC + 1)
                nc.tensor.matmul(bank[2][:, :], wqk[:, 0, :], xnT[:, :], start=True, stop=True).then_inc(q_done, 1)
                wait(pe, up_copied, b * HC + 1)
                nc.tensor.matmul(bank[3][:, :], wqk[:, 1, :], xnT[:, :], start=True, stop=True).then_inc(k_done, 1)
                wait(pe, t1_ready, b * HC + 2)
                for u in range(TB):
                    last = nc.tensor.matmul(bank[4][:, u * P:(u + 1) * P], xnT[:, u * P:(u + 1) * P],
                                            wqkv[:, 2 * D:3 * D], start=True, stop=True)
                last.then_inc(v_done, 1)

            transpose_in(0)
            products(0)
            transpose_in(1)
            down(0)
            products(1)
            with pe.Fori(2, B) as b:
                transpose_in(b)
                down(b - 1)
                products(b)
            down(B - 1)

            def exp_tile(b, g, k):
                wait(pe, exp_done, b * (TILES * NG) + TILES * g + k + 1 - ER)
                if k == 0:
                    wait(pe, shift_in[g % 2], b * 96 + 48 * (g // 2 + 1))
                for col, h, j in exp_blocks(k):
                    last = nc.tensor.matmul(bank[(TILES * g + k) % ER][:, col:col + S - P * j],
                                            KA[:, g, h, P * j:P * (j + 1)], QA[:, g, h, P * j:S],
                                            start=True, stop=True)
                last.then_inc(e_done, 1)

            def max_tile(b, g, k):
                wait(pe, red_done, b * (TILES * NG) + TILES * g + k + 1 - MR)
                slot = g % NG
                if k == 0:
                    wait(pe, aug_in[slot], (b + g // NG) * 32 + 32)
                for col, h, i in max_blocks(k):
                    dst = bank[4 + k % MR]
                    nc.tensor.matmul(dst[:, col:col + P * (i + 1)], QA[0:SHIFT_ROW, slot, h, P * i:P * (i + 1)],
                                     KA[0:SHIFT_ROW, slot, h, 0:P * (i + 1)], start=True, stop=False)
                    last = nc.tensor.matmul(dst[:, col + P * i:col + P * (i + 1)], idh[:, :], maskh[:, :],
                                            start=False, stop=True)
                last.then_inc(m_done, 1)

            def values(b, g, piece):
                j = (0, 1, 3, 2)[piece]
                gg = g % NG
                half, gl = gg // 2, gg % 2
                wait(pe, masked, b * (4 * NG) + 4 * g + piece + 1)
                if piece == 0 and gl == 0:
                    halves = b * 2 + g // 2
                    wait(pe, vb_ready, halves * 2 + 2)
                    wait(pe, o_copied, halves)
                for c in range(GH):
                    last = nc.tensor.matmul(bank[6][32 * c:32 * c + 32, P * j:S], Vb[:, j, half, c, gl, :],
                                            PT[:, gg % 2, c, KEY_COL[j]:KEY_COL[j] + S - P * j],
                                            start=(gl == 0 and piece == 0), stop=(gl == 1 and piece == 3))
                last.then_inc(pv_done, 1)

            def transpose_shift(b, g):
                wait(pe, msp_ready, b * NG + g + 1)
                before = {1: (norm_ready, b * 2 - 1), 2: (mt_copied, b * NG + g), 3: (norm_ready, b * 2),
                          4: (s_ready, b)}[g]
                wait(pe, *before)
                nc.tensor.transpose(bank[7][:, 0:P // 2].bitcast(bf16),
                                    msp[:, :, :].rearrange("p a m -> p (a m)"), idh[:, :]).then_inc(mt_done, 1)

            def transpose_sums(b, half):
                wait(pe, o_copied, b * 2 + half + 1)
                if exists(b, NG):
                    wait(pe, mt_copied, b * NG + 2 * half + 5)
                elif half == 0:
                    wait(pe, s_ready, b)
                else:
                    wait(pe, norm_ready, b * 2 + 1)
                for u in range(TB):
                    last = nc.tensor.transpose(bank[7][:, u * P:(u + 1) * P], OS[:, u * P:(u + 1) * P], idf[:, :])
                last.then_inc(tr_done, 1)

            def transpose_back(b):
                wait(pe, norm_ready, b * 2 + 2)
                if exists(b, NG):
                    wait(pe, mt_copied, b * NG + 8)
                for u in range(TB):
                    last = nc.tensor.transpose(bank[7][:, u * P:(u + 1) * P], AN[:, u, :], idf[:, :])
                last.then_inc(ant_done, 1)

            def project(b):
                wait(pe, at_copied, b + 1)
                for u in range(TB):
                    last = nc.tensor.matmul(bank[7][:, u * P:(u + 1) * P], AT[:, u * P:(u + 1) * P], wp[:, :],
                                            start=True, stop=True)
                last.then_inc(proj_done, 1)

            def step(b, g):
                later = not isinstance(b, int)
                for k in range(TILES):
                    if exists(b, g):
                        exp_tile(b, g, k)
                    if exists(b, g + 2):
                        max_tile(b, g + 2, k)
                    if k in (1, 3, 4, 7) and exists(b, g - 1):
                        values(b, g - 1, (1, 3, 4, 7).index(k))
                    if k == 2 and exists(b, g + 1):
                        transpose_shift(b, g + 1)
                    if k == 5 and g == 1 and (later or b >= 1):
                        transpose_sums(b - 1, 1)
                    if k == 5 and g == 3 and exists(b, g):
                        transpose_sums(b, 0)
                    if k == 5 and g == 2 and (later or b >= 1):
                        transpose_back(b - 1)
                    if k == 8 and g == 2 and (later or b >= 1):
                        project(b - 1)

            pe.wait_ge(g_stored, B)
            pe.wait_ge(k_roped, 3 * B)
            pe.wait_ge(q_roped, 3 * B)
            pe.wait_ge(v_stored, B)
            pe.wait_ge(t1_ready, HC * B)
            pe.wait_ge(up_copied, HC * B)
            pe.wait_ge(pool_prep, 7)
            attention_steps(pe, step)


def kernel(L0_attn_x, L0_attn_w_qkv, L0_attn_w_proj, L0_attn_b_proj, L0_ffn_w_gate, L0_ffn_w_up, L0_ffn_w_down):
    import numpy as np
    import ml_dtypes
    import concourse.bacc as bacc
    from concourse.bass_utils import run_bass_kernel_spmd as run

    freq = (1.0 / np.float32(10000.0) ** (np.arange(0, DH, 2, dtype=np.float32) / np.float32(DH))).astype(np.float32)
    angle = np.arange(S, dtype=np.float32)[None, :] * np.repeat(np.tile(freq, 2), H)[:, None]
    cos = np.cos(angle).astype(np.float32)
    sin = np.sin(angle).astype(np.float32)
    sin[P // 2:] *= np.float32(-1.0)
    rows = np.arange(P)
    consts = {
        "cos_t": cos, "sin_t": sin,
        "ident_f": np.eye(P, dtype=np.float32), "ident_h": np.eye(P, dtype=np.float32).astype(ml_dtypes.bfloat16),
        "mask_h": np.where(rows[None, :] > rows[:, None], MASKED, 0.0).astype(ml_dtypes.bfloat16),
    }
    arrays = {"x": L0_attn_x, "w_qkv": L0_attn_w_qkv, "w_proj": L0_attn_w_proj, "b_proj": L0_attn_b_proj,
              "w_gate": L0_ffn_w_gate, "w_up": L0_ffn_w_up, "w_down": L0_ffn_w_down, **consts}
    arrays = {f"in_{k}": np.ascontiguousarray(a) for k, a in arrays.items()}
    nc = bacc.Bacc("TRN2", target_bir_lowering=False, num_devices=1)
    args = [nc.dram_tensor(k, a.shape, mybir.dt.from_np(a.dtype), kind="ExternalInput").ap()
            for k, a in arrays.items()]
    scratch = nc.dram_tensor("scratch", (B, 2, ROWS, H, S), mybir.dt.bfloat16, kind="Internal").ap()
    out = nc.dram_tensor("out_y", (B, S, D), mybir.dt.float32, kind="ExternalOutput").ap()
    attn_ffn_block(nc, *args, scratch, out)
    r = run(nc, [arrays], core_ids=[0])
    return r.results[0]["out_y"]
```

```python
import concourse.bass as bass
from concourse import mybir
from contextlib import ExitStack

B, S, D = 8, 512, 128
H, DH = 16, 8
HID = 384
P = 128
TB = S // P
NT = B * TB
HC = HID // P
GH = 4
NG = H // GH
GROUPS = B * NG
NPROD = 6
ROWS = NPROD * DH
SHIFT_ROW = 96
PAIRS = ("hml", "hm", "h")
TILES = 10
RING = 3
M_BANK, O_BANK, X_BANK = 3, 6, 7
EPS = 1e-5
MASKED = -1.0e9


def wait(eng, sem, value):
    if isinstance(value, int) and value <= 0:
        return
    eng.wait_ge(sem, value)


def wait_apart(eng, sem, value, met, met_value):
    if not isinstance(value, int):
        value = eng.to_reg(value)
    eng.wait_ge(met, met_value)
    wait(eng, sem, value)


def exists(b, g):
    return not isinstance(b, int) or 0 <= NG * b + g < GROUPS


def attn_ffn_block(nc, x, w_qkv, w_proj, b_proj, w_gate, w_up, w_down,
                   cos_t, sin_t, ident_f, ident_h, mask_h, scratch, out):
    fp32 = mybir.dt.float32
    bf16 = mybir.dt.bfloat16
    i32 = mybir.dt.int32
    ALU = mybir.AluOpType
    ACT = mybir.ActivationFunctionType
    AX = mybir.AxisListType
    SCALE = float(DH) ** -0.5

    x_v = x.rearrange("b (t p) d -> p (b t) d", p=P)
    out_v = out.rearrange("b (t p) d -> p (b t) d", p=P)

    ctx = ExitStack()
    with ctx:
        def sb(name, shape, dt=fp32):
            return ctx.enter_context(nc.sbuf_tensor(name, shape, dt))

        def sem(name):
            return ctx.enter_context(nc.semaphore(name))

        cosT, sinT = sb("cosT", [P, S]), sb("sinT", [P, S])
        idf, idh = sb("idf", [P, P]), sb("idh", [P, P], bf16)
        maskh = sb("maskh", [P, P], bf16)
        wqkv, wqk = sb("wqkv", [P, 3 * D]), sb("wqk", [P, 2, D])
        wp, bias = sb("wp", [P, D]), sb("bias", [P, D])
        wgT, wuT, wdT = sb("wgT", [P, HC, P]), sb("wuT", [P, HC, P]), sb("wdT", [P, HC, P])
        x_all = sb("x_all", [P, NT, D])
        gate_all = sb("gate_all", [P, NT, D])
        v_all = sb("v_all", [P, NT, D])
        stats, t6 = sb("stats", [P, NT, 6]), sb("t6", [P, 5, NT])
        mean, rstd = sb("mean", [P, NT]), sb("rstd", [P, NT])
        xnT = sb("xnT", [P, S])
        thf = sb("thf", [P, S])
        ropc, rops, roped, rest = (sb("ropc", [P, 2, S]), sb("rops", [P, 2, S]),
                                   sb("roped", [P, 2, S]), sb("rest", [P, 2, S]))
        parts = sb("parts", [P, 2, 2, 3, S], bf16)
        QA, KA = sb("QA", [P, NG, GH, S], bf16), sb("KA", [P, NG, GH, S], bf16)
        PT = sb("PT", [P, 2, GH, 1280])
        Vb = sb("Vb", [P, TB, 2, GH, 2, 32])
        rmax, nmax = sb("rmax", [P, 2, GH, TB]), sb("nmax", [P, 3, GH * TB])
        msp, mT = sb("msp", [P, 8, GH * TB], bf16), sb("mT", [3 * GH * TB, 2, P], bf16)
        OS, rl, AN, AT = sb("OS", [P, S]), sb("rl", [P, TB, 8]), sb("AN", [P, TB, D]), sb("AT", [P, S])
        sS, fo = sb("sS", [P, TB, D]), sb("fo", [P, TB, D])
        pt_flat = PT[:, :, :, :].rearrange("p a h c -> p (a h c)")
        xn = pt_flat[:, 0:S].rearrange("p (t d) -> p t d", d=D)
        wi = pt_flat[:, S:S + 3 * HID].bitcast(i32).rearrange("p (w c k) -> p w c k", w=3, c=HC)
        wf = pt_flat[:, S + 3 * HID:S + 6 * HID].rearrange("p (w c k) -> p w c k", w=3, c=HC)

        fo1 = S + 6 * HID
        th, ups, t1, hT = (pt_flat[:, fo1 + i * HC * S:fo1 + (i + 1) * HC * S].rearrange("p (c s) -> p c s", c=HC)
                           for i in range(4))

        bank = [ctx.enter_context(nc.psum_tensor(f"bank{i}", [P, S], fp32)) for i in range(8)]

        idf_in, consts_in, wi_in, x_in = sem("idf_in"), sem("consts_in"), sem("wi_in"), [sem(f"x_in{i}") for i in range(4)]
        dve_prep, pool_prep = sem("dve_prep"), sem("pool_prep")
        var_ready, std_ready, xn_ready = sem("var_ready"), sem("std_ready"), sem("xn_ready")
        wf_ready, wT_done, wT_ready = sem("wf_ready"), sem("wT_done"), sem("wT_ready")
        tp_done, xnT_ready = sem("tp_done"), sem("xnT_ready")
        gate_done, up_done, th_ready, up_copied, t1_ready, h_ready = (
            sem("gate_done"), sem("up_done"), sem("th_ready"), sem("up_copied"), sem("t1_ready"), sem("h_ready"))
        down_done, thf_ready, g_stored = sem("down_done"), sem("thf_ready"), sem("g_stored")
        q_done, k_done, v_done, v_stored = sem("q_done"), sem("k_done"), sem("v_done"), sem("v_stored")
        q_roped, k_roped, roped_ready = sem("q_roped"), sem("k_roped"), sem("roped_ready")
        hi_ready, rest_ready, mid_ready, lo_ready = (
            sem("hi_ready"), sem("rest_ready"), sem("mid_ready"), sem("lo_ready"))
        parts_written = sem("parts_written")
        aug_in = [sem(f"aug_in{i}") for i in range(NG)]
        shift_in = [sem("shift_in0"), sem("shift_in1")]
        e_done, exp_done, m_done, red_done = sem("e_done"), sem("exp_done"), sem("m_done"), sem("red_done")
        masked, pv_done, o_copied, vb_ready = sem("masked"), sem("pv_done"), sem("o_copied"), sem("vb_ready")
        shift_chain, msp_ready, mt_done, mt_copied = (
            sem("shift_chain"), sem("msp_ready"), sem("mt_done"), sem("mt_copied"))
        tr_done, rl_ready, norm_ready, ant_done, at_copied = (
            sem("tr_done"), sem("rl_ready"), sem("norm_ready"), sem("ant_done"), sem("at_copied"))
        proj_done, s_ready, sg_ready, f_ready, out_written = (
            sem("proj_done"), sem("s_ready"), sem("sg_ready"), sem("f_ready"), sem("out_written"))

        block = ctx.enter_context(nc.Block())

        def at_parity(t, b):
            return t[:, b % 2] if isinstance(b, int) else t[:, bass.ds(b % 2, 1)].rearrange("p o q a s -> p (o q) a s")

        def exp_blocks(k):
            if k < 4:
                return [(0, k, 0)]
            if k < 8:
                return [(0, k - 4, 1), (384, k - 4, 3)]
            return [(0, 2 * (k - 8), 2), (256, 2 * (k - 8) + 1, 2)]

        def max_blocks(k):
            pair, r = divmod(k, 5)
            if r < 2:
                return [(0, 2 * pair + r, 3)]
            if r < 4:
                return [(0, 2 * pair + r - 2, 2), (384, 2 * pair + r - 2, 0)]
            return [(0, 2 * pair, 1), (256, 2 * pair + 1, 1)]

        def freed(b, g, k):
            tile = TILES * (g % NG) + k
            return b * (TILES * NG) + TILES * g + k + (0 if tile == 0 else 1 - RING)

        def ring(g, k):
            return (TILES * (g % NG) + k) % RING

        KEY_COL = {0: 0, 1: 512, 3: 896, 2: 1024}

        def attention_steps(eng, step, tail=lambda: None):
            step(-1, 2)
            tail()
            step(-1, 3)
            for g in range(2 * NG):
                step(g // NG, g % NG)
            with eng.Fori(2, B - 1) as b:
                for g in range(NG):
                    step(b, g)
            for g in range(NG):
                step(B - 1, g)
            for g in range(3):
                step(B, g)

        @block.sync
        def _(sp):
            def load_x(i):
                sp.dma_start(x_all[:, 8 * i:8 * i + 8, :], x_v[:, 8 * i:8 * i + 8, :]).then_inc(x_in[i], 16)

            sp.dma_start(wi[:, 0, :, :], w_gate.rearrange("(c p) k -> p c k", p=P)).then_inc(wi_in, 16)
            sp.dma_start(wi[:, 1, :, :], w_up.rearrange("(c p) k -> p c k", p=P)).then_inc(wi_in, 16)
            sp.dma_start(wi[:, 2, :, :], w_down.rearrange("p (c k) -> p c k", c=HC)).then_inc(wi_in, 16)
            for i in range(4):
                load_x(i)

            def write_parts(b):
                wait_apart(sp, parts_written, b * 96, wi_in, 48)
                wait_apart(sp, lo_ready, b + 1, wi_in, 48)
                row = 0
                for n, names in enumerate(PAIRS):
                    m = len(names)
                    dst_q = scratch[b, 0, row:row + m * DH].rearrange("(a d) h t -> (d h) a t", a=m)
                    dst_k = scratch[b, 1, row:row + m * DH].rearrange("(a d) h t -> (d h) a t", a=m)
                    sp.dma_start(dst_q, at_parity(parts, b)[:, 0, 0:m, :]).then_inc(parts_written, 16)
                    sp.dma_start(dst_k, at_parity(parts, b)[:, 1, n:n + 1, :].broadcast_to([P, m, S])).then_inc(parts_written, 16)
                    row += m * DH

            write_parts(0)
            with sp.Fori(1, B - 1) as b:
                write_parts(b)

            def load_aug(b, g):
                if not exists(b, g):
                    return
                bb, slot = b + g // NG, g % NG
                first = (slot // 2) * 8 + slot % 2
                wait_apart(sp, e_done, b * (TILES * NG) + TILES * (g - NG + 1), wi_in, 48)
                for side, dst in ((0, QA), (1, KA)):
                    sp.dma_start(dst[0:ROWS, slot, :, :],
                                 scratch[bb, side, :, first:first + 7:2, :]).then_inc(aug_in[slot], 16)

            def step(b, g):
                load_aug(b, g + 3)
                if exists(b, g + 1):
                    gn = g + 1
                    wait_apart(sp, mt_copied, b * NG + gn + 1, wi_in, 48)
                    wait_apart(sp, e_done, b * (TILES * NG) + TILES * (gn - NG + 1), wi_in, 48)
                    for part in range(3):
                        sp.dma_start(QA[SHIFT_ROW + part:SHIFT_ROW + part + 1, gn % NG, :, :]
                                     .rearrange("o h (i q) -> o (h i) q", q=P),
                                     mT[16 * part:16 * part + 16, gn % 2, :]).then_inc(shift_in[gn % 2], 16)
                if g == 0 and (not isinstance(b, int) or b >= 2):
                    store(b - 2)

            def store(b):
                wait_apart(sp, f_ready, b + 1, wi_in, 48)
                sp.dma_start(out_v[:, bass.ds(b * TB, TB), :], fo[:, :, :]).then_inc(out_written, 16)

            sp.wait_ge(parts_written, 96 * (B - 1))
            sp.wait_ge(pool_prep, 7)
            load_aug(-1, 4)

            def last_parts():
                write_parts(B - 1)
                sp.wait_ge(parts_written, 96 * B)

            attention_steps(sp, step, last_parts)
            store(B - 1)
            wait(sp, out_written, 16 * B)

        @block.gpsimd
        def _(pool):
            nc.gpsimd.memset(QA[:, :, :, :], 0.0).then_inc(pool_prep, 1)
            nc.gpsimd.memset(KA[:, :, :, :], 0.0).then_inc(pool_prep, 1)
            pool.wait_ge(pool_prep, 2)
            nc.gpsimd.memset(KA[SHIFT_ROW:SHIFT_ROW + 3, :, :, :], 1.0).then_inc(pool_prep, 1)
            pool.wait_ge(pool_prep, 3)
            nc.gpsimd.memset(Vb[:, :, :, :, :, :], 0.0).then_inc(pool_prep, 1)
            pool.wait_ge(pool_prep, 4)
            nc.gpsimd.memset(msp[:, 3:8, :], 0.0).then_inc(pool_prep, 1)
            for gl in range(2):
                nc.gpsimd.memset(Vb[:, :, :, :, gl, 16 * gl + DH:16 * gl + 2 * DH], 1.0).then_inc(pool_prep, 1)

            def hidden(b):
                for c in range(HC):
                    wait(pool, t1_ready, b * HC + c + 1)
                    wait(pool, up_copied, b * HC + c + 1)
                    if c == 0:
                        wait(pool, down_done, b)
                    nc.gpsimd.tensor_tensor(hT[:, c, :], t1[:, c, :], ups[:, c, :], ALU.mult).then_inc(h_ready, 1)

            def low_parts(b):
                wait(pool, mid_ready, b + 1)
                nc.gpsimd.tensor_tensor(at_parity(parts, b)[:, :, 2, :], rest[:, :, :],
                                        at_parity(parts, b)[:, :, 1, :],
                                        ALU.subtract).then_inc(lo_ready, 1)

            hidden(0)
            hidden(1)
            low_parts(0)
            with pool.Fori(2, B) as b:
                hidden(b)
                low_parts(b - 1)

            def tail():
                low_parts(B - 1)

            def shift_parts(b, g):
                wait_apart(pool, mt_done, b * NG + g, pool_prep, 7)
                wait_apart(pool, red_done, b * (TILES * NG) + TILES * (g + 1), pool_prep, 7)
                flat = rmax[:, g % 2, :, :].rearrange("p h i -> p (h i)")
                for stage in range(5):
                    if stage == 0:
                        ins = nc.gpsimd.tensor_scalar(nmax[:, 0, :], flat, -1.0, None, ALU.mult)
                    elif stage == 1:
                        ins = nc.gpsimd.tensor_copy(msp[:, 0, :], nmax[:, 0, :])
                    elif stage == 2:
                        ins = nc.gpsimd.tensor_tensor(nmax[:, 1, :], nmax[:, 0, :], msp[:, 0, :], ALU.subtract)
                    elif stage == 3:
                        ins = nc.gpsimd.tensor_copy(msp[:, 1, :], nmax[:, 1, :])
                    else:
                        ins = nc.gpsimd.tensor_tensor(msp[:, 2, :], nmax[:, 1, :], msp[:, 1, :], ALU.subtract)
                    if stage < 4:
                        ins.then_inc(shift_chain, 1)
                        wait_apart(pool, shift_chain, b * (4 * NG) + 4 * g + stage + 1, pool_prep, 7)
                    else:
                        ins.then_inc(msp_ready, 1)

            def step(b, g):
                if g % 2 == 0 and exists(b, g):
                    half = g // 2
                    wait(pool, pv_done, b * (4 * NG) + 4 * (g - 2))
                    wait(pool, v_stored, B)
                    wait(pool, pool_prep, 7)
                    for gl in range(2):
                        src = v_all[:, bass.ds(b * TB, TB), :].rearrange(
                            "p t (f c a d) -> p t f c a d", f=2, c=GH, a=2)[:, :, half, :, gl, :]
                        nc.gpsimd.tensor_copy(Vb[:, :, half, :, gl, 16 * gl:16 * gl + DH], src).then_inc(vb_ready, 1)
                if exists(b, g):
                    par = g % 2
                    for j, after in ((0, 4), (1, 8), (3, 8), (2, 10)):
                        wait_apart(pool, exp_done, b * (TILES * NG) + TILES * g + after, pool_prep, 7)
                        blk = PT[:, par, :, KEY_COL[j]:KEY_COL[j] + P]
                        nc.gpsimd.affine_select(out=blk, in_=blk, compare_op=ALU.is_ge, fill=0.0, base=0,
                                                pattern=[[0, GH], [1, P]],
                                                channel_multiplier=-1).then_inc(masked, 1)
                if exists(b, g + 2):
                    shift_parts(b, g + 2)
                if g == 3 and (not isinstance(b, int) or 1 <= b < B):
                    finish(b - 1)

            def finish(b):
                wait(pool, s_ready, b + 1)
                pool.wait_ge(g_stored, B)
                wait(pool, out_written, b * 16)
                nc.gpsimd.tensor_tensor(sS[:, :, :], sS[:, :, :], gate_all[:, bass.ds(b * TB, TB), :],
                                        ALU.mult).then_inc(sg_ready, 1)
                wait(pool, sg_ready, b + 1)
                nc.gpsimd.tensor_tensor(fo[:, :, :], sS[:, :, :], x_all[:, bass.ds(b * TB, TB), :],
                                        ALU.add).then_inc(f_ready, 1)

            attention_steps(pool, step, tail)
            finish(B - 1)

        @block.scalar
        def _(act):
            act.dma_start(idf[:, :], ident_f).then_inc(idf_in, 16)
            for dst, src in ((wqkv[:, :], w_qkv), (wp[:, :], w_proj),
                             (bias[:, :], b_proj.rearrange("(o d) -> o d", o=1).broadcast_to([P, D])),
                             (cosT[:, :], cos_t), (sinT[:, :], sin_t), (idh[:, :], ident_h),
                             (maskh[:, :], mask_h)):
                act.dma_start(dst, src).then_inc(consts_in, 16)
            act.wait_ge(var_ready, 1)
            first = rstd[:, 0:2 * TB]
            nc.scalar.activation(first, first, ACT.Sqrt).then_inc(std_ready, 1)
            for w, dst in enumerate((wgT, wuT, wdT)):
                act.wait_ge(wT_done, w + 1)
                nc.scalar.activation(dst[:, :, :].rearrange("p c k -> p (c k)"), bank[2 + w][:, 0:HID],
                                     ACT.Copy, scale=0.5 if w == 2 else 1.0).then_inc(wT_ready, 1)

            def normed(b):
                wait(act, tp_done, b + 1)
                wait(act, v_done, b)
                nc.scalar.activation(xnT[:, :], bank[0][:, :], ACT.Copy).then_inc(xnT_ready, 1)

            def outer_tanh(b):
                wait(act, down_done, b + 1)
                wait(act, g_stored, b)
                nc.scalar.activation(thf[:, :], bank[1][:, :], ACT.Tanh, scale=0.5).then_inc(thf_ready, 1)

            def chunk(b, c):
                wait(act, gate_done, b * HC + c + 1)
                wait(act, t1_ready, (b - 1) * HC + c + 1)
                nc.scalar.activation(th[:, c, :], bank[2 + 2 * c][:, :], ACT.Tanh, scale=0.5).then_inc(th_ready, 1)
                wait(act, up_done, b * HC + c + 1)
                wait(act, h_ready, (b - 1) * HC + c + 1)
                nc.scalar.activation(ups[:, c, :], bank[3 + 2 * c][:, :], ACT.Copy).then_inc(up_copied, 1)

            def high_parts(b):
                wait(act, roped_ready, b + 1)
                wait(act, parts_written, (b - 1) * 96)
                nc.scalar.activation(at_parity(parts, b)[:, :, 0, :], roped[:, :, :], ACT.Copy).then_inc(hi_ready, 1)

            def mid_parts(b):
                wait(act, rest_ready, b + 1)
                nc.scalar.activation(at_parity(parts, b)[:, :, 1, :], rest[:, :, :], ACT.Copy).then_inc(mid_ready, 1)

            def store_v(b):
                wait(act, v_done, b + 1)
                nc.scalar.activation(v_all[:, bass.ds(b * TB, TB), :].rearrange("p t d -> p (t d)"),
                                     bank[4][:, :], ACT.Copy).then_inc(v_stored, 1)

            def batch(b, first):
                normed(b)
                if first:
                    others = rstd[:, 2 * TB:NT]
                    act.wait_ge(var_ready, 2)
                    nc.scalar.activation(others, others, ACT.Sqrt).then_inc(std_ready, 1)
                else:
                    outer_tanh(b - 1)
                chunk(b, 0)
                if not first:
                    high_parts(b - 1)
                chunk(b, 1)
                if not first:
                    mid_parts(b - 1)
                chunk(b, 2)
                store_v(b)

            batch(0, True)
            batch(1, False)
            batch(2, False)
            with act.Fori(3, B) as b:
                batch(b, False)

            def tail():
                high_parts(B - 1)
                mid_parts(B - 1)
                outer_tanh(B - 1)

            def copy_shift(b, g):
                wait(act, mt_done, b * NG + g + 1)
                wait(act, shift_in[g % 2], b * 96 + 48 * ((g - 2) // 2 + 1))
                nc.scalar.activation(mT[:, g % 2, :], bank[X_BANK][0:3 * GH * TB, 0:P // 2].bitcast(bf16),
                                     ACT.Copy).then_inc(mt_copied, 1)

            def copy_o(b, half):
                wait(act, pv_done, b * (4 * NG) + 8 * half + 8)
                wait(act, tr_done, b * 2 + half)
                nc.scalar.activation(OS[:, :], bank[O_BANK][:, :], ACT.Copy).then_inc(o_copied, 1)

            def step(b, g):
                for k in range(TILES):
                    if exists(b, g):
                        n = b * (TILES * NG) + TILES * g + k
                        wait(act, e_done, n + 1)
                        if k == 0:
                            wait(act, pv_done, b * (4 * NG) + 4 * (g - 1))
                        src = bank[ring(g, k)][:, :]
                        if k < 4:
                            dst = PT[:, g % 2, k, 0:512]
                        elif k < 8:
                            dst = PT[:, g % 2, k - 4, 512:1024]
                        else:
                            dst = PT[:, g % 2, 2 * (k - 8):2 * (k - 8) + 2, 1024:1280]
                            src = src.rearrange("p (h q) -> p h q", h=2)
                        nc.scalar.activation(dst, src, ACT.Exp, scale=SCALE).then_inc(exp_done, 1)
                    if k == 4 and exists(b, g + 1):
                        copy_shift(b, g + 1)
                    if k == 7 and g == 2 and (not isinstance(b, int) or b >= 1):
                        wait(act, ant_done, b)
                        wait(act, proj_done, b - 1)
                        nc.scalar.activation(AT[:, :], bank[X_BANK][:, :], ACT.Copy).then_inc(at_copied, 1)
                if g == 0 and (not isinstance(b, int) or b >= 1):
                    copy_o(b - 1, 1)
                if g == 2 and exists(b, g) and (not isinstance(b, int) or b >= 0):
                    copy_o(b, 0)

            attention_steps(act, step, tail)

        @block.vector
        def _(dve):
            dve.wait_ge(wi_in, 48)
            for w in range(3):
                nc.vector.tensor_scalar(wf[:, w, :, :], wi[:, w, :, :], 1.0 / 127.0, None,
                                        ALU.mult).then_inc(wf_ready, 1)
            n = [0]

            def link(ins):
                n[0] += 1
                ins.then_inc(dve_prep, 1)
                dve.wait_ge(dve_prep, n[0])

            def statistics(first, last):
                for i in range(first // 2, last // 2):
                    dve.wait_ge(x_in[i], 16)
                    with dve.Fori(2 * i, 2 * i + 2) as b:
                        for u in range(TB):
                            nc.vector.bn_stats(stats[:, b * TB + u, :], x_all[:, b * TB + u, :]).then_inc(dve_prep, 1)
                n[0] += (last - first) * TB
                dve.wait_ge(dve_prep, n[0])
                r = slice(first * TB, last * TB)
                me, se, mo, so = (stats[:, r, i] for i in (1, 2, 4, 5))
                nc.vector.tensor_tensor(t6[:, 0, r], me, mo, ALU.add).then_inc(dve_prep, 1)
                nc.vector.tensor_tensor(t6[:, 1, r], me, mo, ALU.subtract).then_inc(dve_prep, 1)
                nc.vector.tensor_tensor(t6[:, 2, r], se, so, ALU.add).then_inc(dve_prep, 1)
                n[0] += 3
                dve.wait_ge(dve_prep, n[0])
                nc.vector.tensor_scalar(mean[:, r], t6[:, 0, r], 0.5, None, ALU.mult).then_inc(dve_prep, 1)
                nc.vector.tensor_tensor(t6[:, 3, r], t6[:, 1, r], t6[:, 1, r], ALU.mult).then_inc(dve_prep, 1)
                nc.vector.tensor_scalar(t6[:, 4, r], t6[:, 2, r], 1.0 / D, EPS, ALU.mult,
                                        ALU.add).then_inc(dve_prep, 1)
                n[0] += 3
                dve.wait_ge(dve_prep, n[0])
                nc.vector.scalar_tensor_tensor(out=rstd[:, r], in0=t6[:, 3, r], scalar=0.25, in1=t6[:, 4, r],
                                               op0=ALU.mult, op1=ALU.add).then_inc(var_ready, 1)

            def invert(first, last, count):
                dve.wait_ge(std_ready, count)
                link(nc.vector.reciprocal(rstd[:, first * TB:last * TB], rstd[:, first * TB:last * TB]))

            statistics(0, 2)
            dve.wait_ge(consts_in, 7 * 16)
            for i in range(2):
                nc.vector.tensor_copy(wqk[:, i, :].rearrange("p (d h) -> p d h", d=DH),
                                      wqkv[:, i * D:(i + 1) * D].rearrange("p (h d) -> p d h", d=DH)
                                      ).then_inc(wf_ready, 1)
            link(nc.vector.tensor_scalar(wp[:, :], wp[:, :], 0.5, None, ALU.mult))
            link(nc.vector.tensor_scalar(bias[:, :], bias[:, :], 0.5, None, ALU.mult))
            invert(0, 2, 1)

            def normalise_in(b):
                wait(dve, tp_done, b)
                for u in range(TB):
                    last = nc.vector.tensor_scalar(xn[:, u, :], x_all[:, b * TB + u, :],
                                                   mean[:, bass.ds(b * TB + u, 1)],
                                                   rstd[:, bass.ds(b * TB + u, 1)], ALU.subtract, ALU.mult)
                last.then_inc(xn_ready, 1)

            def outer_gate(b):
                wait(dve, thf_ready, b + 1)
                nc.vector.scalar_tensor_tensor(out=gate_all[:, bass.ds(b * TB, TB), :].rearrange("p t d -> p (t d)"),
                                               in0=thf[:, :], scalar=1.0, in1=bank[1][:, :],
                                               op0=ALU.add, op1=ALU.mult).then_inc(g_stored, 1)

            def gate(b, c):
                wait(dve, th_ready, b * HC + c + 1)
                wait(dve, h_ready, (b - 1) * HC + c + 1)
                nc.vector.scalar_tensor_tensor(out=t1[:, c, :], in0=th[:, c, :], scalar=1.0, in1=bank[2 + 2 * c][:, :],
                                               op0=ALU.add, op1=ALU.mult).then_inc(t1_ready, 1)

            def rest_of(b):
                wait(dve, hi_ready, b + 1)
                wait(dve, lo_ready, b)
                nc.vector.tensor_tensor(rest[:, :, :], roped[:, :, :], at_parity(parts, b)[:, :, 0, :],
                                        ALU.subtract).then_inc(rest_ready, 1)

            def rope(b):
                for i, (done, roped_sem) in enumerate(((q_done, q_roped), (k_done, k_roped))):
                    wait(dve, done, b + 1)
                    if i == 0:
                        wait(dve, roped_ready, b)
                    nc.vector.tensor_tensor(ropc[:, i, :], bank[2 + i][:, :], cosT[:, :],
                                            ALU.mult).then_inc(roped_sem, 1)
                    nc.vector.tensor_tensor(rops[0:64, i, :], bank[2 + i][64:128, :], sinT[64:128, :],
                                            ALU.mult).then_inc(roped_sem, 1)
                    nc.vector.tensor_tensor(rops[64:128, i, :], bank[2 + i][0:64, :], sinT[0:64, :],
                                            ALU.mult).then_inc(roped_sem, 1)
                wait(dve, q_roped, b * 3 + 3)
                wait(dve, k_roped, b * 3 + 3)
                wait(dve, rest_ready, b)
                nc.vector.tensor_tensor(roped[:, :, :], ropc[:, :, :], rops[:, :, :],
                                        ALU.add).then_inc(roped_ready, 1)

            def batch(b, first, last=False):
                if not first:
                    outer_gate(b - 1)
                if not last:
                    normalise_in(b + 1)
                gate(b, 0)
                if not first:
                    rest_of(b - 1)
                gate(b, 1)
                gate(b, 2)
                rope(b)

            normalise_in(0)
            statistics(2, B)
            invert(2, B, 2)
            batch(0, True)
            batch(1, False)
            with dve.Fori(2, B - 1) as b:
                batch(b, False)
            batch(B - 1, False, True)

            def tail():
                rest_of(B - 1)
                outer_gate(B - 1)

            def normalise(b, half):
                wait(dve, tr_done, b * 2 + half + 1)
                v = bank[X_BANK][:, :].rearrange("p (t e w) -> p t e w", t=TB, w=2 * DH)
                nc.vector.reciprocal(rl[:, :, :], v[:, :, :, DH]).then_inc(rl_ready, 1)
                wait(dve, rl_ready, b * 2 + half + 1)
                wait(dve, ant_done, b)
                nc.vector.tensor_tensor(AN[:, :, 64 * half:64 * half + 64].rearrange("p t (e d) -> p t e d", d=DH),
                                        v[:, :, :, 0:DH],
                                        rl[:, :, :].rearrange("p t (e o) -> p t e o", o=1).broadcast_to([P, TB, 8, DH]),
                                        ALU.mult).then_inc(norm_ready, 1)

            def projected(b):
                wait(dve, proj_done, b + 1)
                wait(dve, f_ready, b)
                nc.vector.tensor_tensor(sS[:, :, :], bank[X_BANK][:, :].rearrange("p (t d) -> p t d", t=TB),
                                        bias[:, :].rearrange("p (o d) -> p o d", o=1).broadcast_to([P, TB, D]),
                                        ALU.add).then_inc(s_ready, 1)

            def step(b, g):
                later = not isinstance(b, int)
                for k in range(TILES):
                    if exists(b, g + 2):
                        n = b * (TILES * NG) + TILES * (g + 2) + k
                        wait(dve, m_done, n + 1)
                        if k == 0:
                            wait(dve, msp_ready, b * NG + g + 1)
                        src = bank[M_BANK + ring(g + 2, k)]
                        blocks = max_blocks(k)
                        if blocks[0][2] == 1:
                            last = nc.vector.tensor_reduce(rmax[:, g % 2, blocks[0][1]:blocks[0][1] + 2, 1],
                                                           src[:, :].rearrange("p (h q) -> p h q", h=2), AX.X, ALU.max)
                        else:
                            for col, h, i in blocks:
                                last = nc.vector.tensor_reduce(rmax[:, g % 2, h, i:i + 1], src[:, col:col + P * (i + 1)],
                                                               AX.X, ALU.max)
                        last.then_inc(red_done, 1)
                    if k == 6 and g == 1 and (later or b >= 1):
                        normalise(b - 1, 1)
                    if k == 6 and g == 3 and exists(b, g):
                        normalise(b, 0)
                    if k == 9 and g == 2 and (later or b >= 1):
                        projected(b - 1)

            attention_steps(dve, step, tail)

        @block.tensor
        def _(pe):
            pe.wait_ge(idf_in, 16)
            pe.wait_ge(wf_ready, 3)
            for w in range(3):
                for c in range(HC):
                    last = nc.tensor.transpose(bank[2 + w][:, c * P:(c + 1) * P], wf[:, w, c, :], idf[:, :])
                last.then_inc(wT_done, 1)
            pe.wait_ge(wT_ready, 3)
            pe.wait_ge(consts_in, 7 * 16)
            pe.wait_ge(wf_ready, 5)

            def transpose_in(b):
                wait(pe, xn_ready, b + 1)
                wait(pe, xnT_ready, b)
                for u in range(TB):
                    last = nc.tensor.transpose(bank[0][:, u * P:(u + 1) * P], xn[:, u, :], idf[:, :])
                last.then_inc(tp_done, 1)

            def down(b):
                wait(pe, h_ready, (b + 1) * HC)
                wait(pe, g_stored, b)
                for u in range(TB):
                    for c in range(HC):
                        last = nc.tensor.matmul(bank[1][:, u * P:(u + 1) * P], hT[:, c, u * P:(u + 1) * P],
                                                wdT[:, c, :], start=(c == 0), stop=(c == HC - 1))
                last.then_inc(down_done, 1)

            def products(b):
                wait(pe, xnT_ready, b + 1)
                free_gate = ((q_roped, b * 3), (v_stored, b), (t1_ready, b * HC))
                free_up = ((k_roped, b * 3), (up_copied, (b - 1) * HC + 2), (up_copied, b * HC))
                for c in range(HC):
                    wait(pe, *free_gate[c])
                    nc.tensor.matmul(bank[2 + 2 * c][:, :], wgT[:, c, :], xnT[:, :], start=True,
                                     stop=True).then_inc(gate_done, 1)
                    wait(pe, *free_up[c])
                    nc.tensor.matmul(bank[3 + 2 * c][:, :], wuT[:, c, :], xnT[:, :], start=True,
                                     stop=True).then_inc(up_done, 1)
                wait(pe, t1_ready, b * HC + 1)
                nc.tensor.matmul(bank[2][:, :], wqk[:, 0, :], xnT[:, :], start=True, stop=True).then_inc(q_done, 1)
                wait(pe, up_copied, b * HC + 1)
                nc.tensor.matmul(bank[3][:, :], wqk[:, 1, :], xnT[:, :], start=True, stop=True).then_inc(k_done, 1)
                wait(pe, t1_ready, b * HC + 2)
                for u in range(TB):
                    last = nc.tensor.matmul(bank[4][:, u * P:(u + 1) * P], xnT[:, u * P:(u + 1) * P],
                                            wqkv[:, 2 * D:3 * D], start=True, stop=True)
                last.then_inc(v_done, 1)

            transpose_in(0)
            products(0)
            transpose_in(1)
            down(0)
            products(1)
            with pe.Fori(2, B) as b:
                transpose_in(b)
                down(b - 1)
                products(b)

            def tail():
                down(B - 1)

            def exp_tile(b, g, k):
                wait(pe, exp_done, freed(b, g, k))
                if k == 0:
                    wait(pe, shift_in[g % 2], b * 96 + 48 * (g // 2 + 1))
                for col, h, j in exp_blocks(k):
                    last = nc.tensor.matmul(bank[ring(g, k)][:, col:col + S - P * j],
                                            KA[:, g, h, P * j:P * (j + 1)], QA[:, g, h, P * j:S],
                                            start=True, stop=True)
                last.then_inc(e_done, 1)

            def max_tile(b, g, k):
                wait(pe, red_done, freed(b, g, k))
                slot = g % NG
                if k == 0:
                    wait(pe, aug_in[slot], (b + g // NG) * 32 + 32)
                for col, h, i in max_blocks(k):
                    dst = bank[M_BANK + ring(g, k)]
                    nc.tensor.matmul(dst[:, col:col + P * (i + 1)], QA[0:SHIFT_ROW, slot, h, P * i:P * (i + 1)],
                                     KA[0:SHIFT_ROW, slot, h, 0:P * (i + 1)], start=True, stop=False)
                    last = nc.tensor.matmul(dst[:, col + P * i:col + P * (i + 1)], idh[:, :], maskh[:, :],
                                            start=False, stop=True)
                last.then_inc(m_done, 1)

            def values(b, g, piece):
                j = (0, 1, 3, 2)[piece]
                gg = g % NG
                half, gl = gg // 2, gg % 2
                wait(pe, masked, b * (4 * NG) + 4 * g + piece + 1)
                if piece == 0 and gl == 0:
                    halves = b * 2 + g // 2
                    wait(pe, vb_ready, halves * 2 + 2)
                    wait(pe, o_copied, halves)
                for c in range(GH):
                    last = nc.tensor.matmul(bank[O_BANK][32 * c:32 * c + 32, P * j:S], Vb[:, j, half, c, gl, :],
                                            PT[:, gg % 2, c, KEY_COL[j]:KEY_COL[j] + S - P * j],
                                            start=(gl == 0 and piece == 0), stop=(gl == 1 and piece == 3))
                last.then_inc(pv_done, 1)

            def transpose_shift(b, g):
                wait(pe, msp_ready, b * NG + g + 1)
                before = {1: (norm_ready, b * 2 - 1), 2: (mt_copied, b * NG + g), 3: (norm_ready, b * 2),
                          4: (s_ready, b)}[g]
                wait(pe, *before)
                nc.tensor.transpose(bank[X_BANK][:, 0:P // 2].bitcast(bf16),
                                    msp[:, :, :].rearrange("p a m -> p (a m)"), idh[:, :]).then_inc(mt_done, 1)

            def transpose_sums(b, half):
                wait(pe, o_copied, b * 2 + half + 1)
                if exists(b, NG):
                    wait(pe, mt_copied, b * NG + 2 * half + 5)
                elif half == 0:
                    wait(pe, s_ready, b)
                else:
                    wait(pe, norm_ready, b * 2 + 1)
                for u in range(TB):
                    last = nc.tensor.transpose(bank[X_BANK][:, u * P:(u + 1) * P], OS[:, u * P:(u + 1) * P], idf[:, :])
                last.then_inc(tr_done, 1)

            def transpose_back(b):
                wait(pe, norm_ready, b * 2 + 2)
                if exists(b, NG):
                    wait(pe, mt_copied, b * NG + 8)
                for u in range(TB):
                    last = nc.tensor.transpose(bank[X_BANK][:, u * P:(u + 1) * P], AN[:, u, :], idf[:, :])
                last.then_inc(ant_done, 1)

            def project(b):
                wait(pe, at_copied, b + 1)
                for u in range(TB):
                    last = nc.tensor.matmul(bank[X_BANK][:, u * P:(u + 1) * P], AT[:, u * P:(u + 1) * P], wp[:, :],
                                            start=True, stop=True)
                last.then_inc(proj_done, 1)

            def step(b, g):
                later = not isinstance(b, int)
                for k in range(TILES):
                    if exists(b, g):
                        exp_tile(b, g, k)
                    if exists(b, g + 2):
                        max_tile(b, g + 2, k)
                    if k in (1, 3, 4, 7) and exists(b, g - 1):
                        values(b, g - 1, (1, 3, 4, 7).index(k))
                    if k == 3 and exists(b, g + 1):
                        transpose_shift(b, g + 1)
                    if k == 6 and g == 1 and (later or b >= 1):
                        transpose_sums(b - 1, 1)
                    if k == 6 and g == 3 and exists(b, g):
                        transpose_sums(b, 0)
                    if k == 6 and g == 2 and (later or b >= 1):
                        transpose_back(b - 1)
                    if k == 9 and g == 2 and (later or b >= 1):
                        project(b - 1)

            pe.wait_ge(k_roped, 3 * B)
            pe.wait_ge(q_roped, 3 * B)
            pe.wait_ge(v_stored, B)
            pe.wait_ge(t1_ready, HC * B)
            pe.wait_ge(up_copied, HC * B)
            pe.wait_ge(pool_prep, 7)
            attention_steps(pe, step, tail)


def kernel(L0_attn_x, L0_attn_w_qkv, L0_attn_w_proj, L0_attn_b_proj, L0_ffn_w_gate, L0_ffn_w_up, L0_ffn_w_down):
    import numpy as np
    import ml_dtypes
    import concourse.bacc as bacc
    from concourse.bass_utils import run_bass_kernel_spmd as run

    freq = (1.0 / np.float32(10000.0) ** (np.arange(0, DH, 2, dtype=np.float32) / np.float32(DH))).astype(np.float32)
    angle = np.arange(S, dtype=np.float32)[None, :] * np.repeat(np.tile(freq, 2), H)[:, None]
    cos = np.cos(angle).astype(np.float32)
    sin = np.sin(angle).astype(np.float32)
    sin[P // 2:] *= np.float32(-1.0)
    rows = np.arange(P)
    consts = {
        "cos_t": cos, "sin_t": sin,
        "ident_f": np.eye(P, dtype=np.float32), "ident_h": np.eye(P, dtype=np.float32).astype(ml_dtypes.bfloat16),
        "mask_h": np.where(rows[None, :] > rows[:, None], MASKED, 0.0).astype(ml_dtypes.bfloat16),
    }
    arrays = {"x": L0_attn_x, "w_qkv": L0_attn_w_qkv, "w_proj": L0_attn_w_proj, "b_proj": L0_attn_b_proj,
              "w_gate": L0_ffn_w_gate, "w_up": L0_ffn_w_up, "w_down": L0_ffn_w_down, **consts}
    arrays = {f"in_{k}": np.ascontiguousarray(a) for k, a in arrays.items()}
    nc = bacc.Bacc("TRN2", target_bir_lowering=False, num_devices=1)
    args = [nc.dram_tensor(k, a.shape, mybir.dt.from_np(a.dtype), kind="ExternalInput").ap()
            for k, a in arrays.items()]
    scratch = nc.dram_tensor("scratch", (B, 2, ROWS, H, S), mybir.dt.bfloat16, kind="Internal").ap()
    out = nc.dram_tensor("out_y", (B, S, D), mybir.dt.float32, kind="ExternalOutput").ap()
    attn_ffn_block(nc, *args, scratch, out)
    r = run(nc, [arrays], core_ids=[0])
    return r.results[0]["out_y"]
```

```python
import concourse.bass as bass
from concourse import mybir
from contextlib import ExitStack

B, S, D = 8, 512, 128
H, DH = 16, 8
HID = 384
P = 128
TB = S // P
NT = B * TB
HC = HID // P
GH = 4
NG = H // GH
GROUPS = B * NG
NPROD = 6
ROWS = NPROD * DH
SHIFT_ROW = ROWS
SHIFTS = 3
MASK_ROW = 64
HALF = P // 2
PAIRS = ("hml", "hm", "h")
TILES = 10
RING = 3
M_BANK, O_BANK, X_BANK = 3, 6, 7
EPS = 1e-5
MASKED = -1.0e9


def wait(eng, sem, value):
    if isinstance(value, int) and value <= 0:
        return
    eng.wait_ge(sem, value)


def wait_apart(eng, sem, value, met, met_value):
    if not isinstance(value, int):
        value = eng.to_reg(value)
    eng.wait_ge(met, met_value)
    wait(eng, sem, value)


def exists(b, g):
    return not isinstance(b, int) or 0 <= NG * b + g < GROUPS


def attn_ffn_block(nc, x, w_qkv, w_proj, b_proj, w_gate, w_up, w_down,
                   cos_t, sin_t, ident_f, ident_h, fixed_rows, zero_rows, scratch, out):
    fp32 = mybir.dt.float32
    bf16 = mybir.dt.bfloat16
    i32 = mybir.dt.int32
    ALU = mybir.AluOpType
    ACT = mybir.ActivationFunctionType
    AX = mybir.AxisListType
    SCALE = float(DH) ** -0.5

    x_v = x.rearrange("b (t p) d -> p (b t) d", p=P)
    out_v = out.rearrange("b (t p) d -> p (b t) d", p=P)

    ctx = ExitStack()
    with ctx:
        def sb(name, shape, dt=fp32):
            return ctx.enter_context(nc.sbuf_tensor(name, shape, dt))

        def sem(name):
            return ctx.enter_context(nc.semaphore(name))

        cosT, sinT = sb("cosT", [P, S]), sb("sinT", [P, S])
        idf, idh = sb("idf", [P, P]), sb("idh", [P, P], bf16)
        wqkv, wqk = sb("wqkv", [P, 3 * D]), sb("wqk", [P, 2, D])
        wp, bias = sb("wp", [P, D]), sb("bias", [P, D])
        wgT, wuT, wdT = sb("wgT", [P, HC, P]), sb("wuT", [P, HC, P]), sb("wdT", [P, HC, P])
        x_all = sb("x_all", [P, NT, D])
        gate_all = sb("gate_all", [P, NT, D])
        v_all = sb("v_all", [P, NT, D])
        stats, t6 = sb("stats", [P, NT, 6]), sb("t6", [P, 5, NT])
        mean, rstd, offset = sb("mean", [P, NT]), sb("rstd", [P, NT]), sb("offset", [P, NT])
        xnT = sb("xnT", [P, S])
        thf = sb("thf", [P, S])
        ropc, rops, roped, rest = (sb("ropc", [P, 2, S]), sb("rops", [P, 2, S]),
                                   sb("roped", [P, 2, S]), sb("rest", [P, 2, S]))
        parts = sb("parts", [P, 2, 2, 3, S], bf16)
        QA, QL, QH, KA = (sb(name, [P, NG, GH, S], bf16) for name in ("QA", "QL", "QH", "KA"))
        PT = sb("PT", [P, 2, GH, 1280])
        Vb = sb("Vb", [P, TB, 2, GH, 2, 32])
        rmax, rmid = sb("rmax", [P, 2, GH, TB]), sb("rmid", [P, GH * TB])
        msp, mT = sb("msp", [P, 8, GH * TB], bf16), sb("mT", [3 * GH * TB, 2, P], bf16)
        rl = sb("rl", [P, TB, 8])
        OS, AT, AN = ropc[:, 0, :], ropc[:, 1, :], xnT[:, :].rearrange("p (t d) -> p t d", t=TB)
        sS, fo = (rops[:, i, :].rearrange("p (t d) -> p t d", t=TB) for i in range(2))
        pt_flat = PT[:, :, :, :].rearrange("p a h c -> p (a h c)")
        xn = pt_flat[:, 0:S].rearrange("p (t d) -> p t d", d=D)
        wi = pt_flat[:, S:S + 3 * HID].bitcast(i32).rearrange("p (w c k) -> p w c k", w=3, c=HC)
        wf = pt_flat[:, S + 3 * HID:S + 6 * HID].rearrange("p (w c k) -> p w c k", w=3, c=HC)
        ffn_at = S + 6 * HID
        th, ups, t1, hT = (pt_flat[:, ffn_at + i * HC * S:ffn_at + (i + 1) * HC * S].rearrange("p (c s) -> p c s", c=HC)
                           for i in range(4))

        bank = [ctx.enter_context(nc.psum_tensor(f"bank{i}", [P, S], fp32)) for i in range(8)]

        idf_in, consts_in, wi_in, x_in = sem("idf_in"), sem("consts_in"), sem("wi_in"), [sem(f"x_in{i}") for i in range(4)]
        dve_prep, pool_prep = sem("dve_prep"), sem("pool_prep")
        var_ready, std_ready, norm_set, xn_ready = (
            sem("var_ready"), sem("std_ready"), sem("norm_set"), sem("xn_ready"))
        wf_ready, wT_done, wT_ready = sem("wf_ready"), sem("wT_done"), sem("wT_ready")
        tp_done, xnT_ready = sem("tp_done"), sem("xnT_ready")
        gate_done, up_done, th_ready, up_copied, t1_ready, h_ready = (
            sem("gate_done"), sem("up_done"), sem("th_ready"), sem("up_copied"), sem("t1_ready"), sem("h_ready"))
        down_done, thf_ready, g_stored = sem("down_done"), sem("thf_ready"), sem("g_stored")
        q_done, k_done, v_done, v_stored = sem("q_done"), sem("k_done"), sem("v_done"), sem("v_stored")
        q_roped, k_roped, roped_ready = sem("q_roped"), sem("k_roped"), sem("roped_ready")
        hi_ready, rest_ready, mid_ready, lo_ready = (
            sem("hi_ready"), sem("rest_ready"), sem("mid_ready"), sem("lo_ready"))
        parts_written, fixed_in, zeros_in = sem("parts_written"), sem("fixed_in"), sem("zeros_in")
        aug_in = [sem(f"aug_in{i}") for i in range(NG)]
        shift_in = [sem("shift_in0"), sem("shift_in1")]
        e_done, exp_done, m_done, red_done = sem("e_done"), sem("exp_done"), sem("m_done"), sem("red_done")
        masked, pv_done, o_copied, vb_ready = sem("masked"), sem("pv_done"), sem("o_copied"), sem("vb_ready")
        shift_chain, msp_ready, mt_done, mt_copied = (
            sem("shift_chain"), sem("msp_ready"), sem("mt_done"), sem("mt_copied"))
        tr_done, rl_ready, norm_ready, ant_done, at_copied = (
            sem("tr_done"), sem("rl_ready"), sem("norm_ready"), sem("ant_done"), sem("at_copied"))
        proj_done, s_ready, sg_ready, f_ready, out_written = (
            sem("proj_done"), sem("s_ready"), sem("sg_ready"), sem("f_ready"), sem("out_written"))

        block = ctx.enter_context(nc.Block())

        def at_parity(t, b):
            return t[:, b % 2] if isinstance(b, int) else t[:, bass.ds(b % 2, 1)].rearrange("p o q a s -> p (o q) a s")

        def exp_blocks(k):
            if k < 4:
                return [(0, k, 0)]
            if k < 8:
                return [(0, k - 4, 1), (384, k - 4, 3)]
            return [(0, 2 * (k - 8), 2), (256, 2 * (k - 8) + 1, 2)]

        def max_blocks(k):
            pair, r = divmod(k, 5)
            if r < 2:
                return [(0, 2 * pair + r, 3)]
            if r < 4:
                return [(0, 2 * pair + r - 2, 2), (384, 2 * pair + r - 2, 0)]
            return [(0, 2 * pair, 1), (256, 2 * pair + 1, 1)]

        in_ring = [t % RING for t in range(TILES * NG - 1)] + [1]

        def ring(g, k):
            return in_ring[TILES * (g % NG) + k]

        def freed(b, g, k):
            tile = TILES * (g % NG) + k
            back = next(d for d in range(1, TILES * NG) if in_ring[tile - d] == in_ring[tile])
            return b * (TILES * NG) + TILES * g + k + 1 - back

        KEY_COL = {0: 0, 1: 512, 3: 896, 2: 1024}

        def attention_steps(eng, step, tail=lambda: None):
            step(-1, 2)
            tail()
            step(-1, 3)
            for g in range(2 * NG):
                step(g // NG, g % NG)
            with eng.Fori(2, B - 1) as b:
                for g in range(NG):
                    step(b, g)
            for g in range(NG):
                step(B - 1, g)
            for g in range(3):
                step(B, g)

        @block.sync
        def _(sp):
            def load_x(i):
                sp.dma_start(x_all[:, 8 * i:8 * i + 8, :], x_v[:, 8 * i:8 * i + 8, :]).then_inc(x_in[i], 16)

            load_x(0)
            sp.dma_start(wi[:, 0, :, :], w_gate.rearrange("(c p) k -> p c k", p=P)).then_inc(wi_in, 16)
            sp.dma_start(wi[:, 1, :, :], w_up.rearrange("(c p) k -> p c k", p=P)).then_inc(wi_in, 16)
            sp.dma_start(wi[:, 2, :, :], w_down.rearrange("p (c k) -> p c k", c=HC)).then_inc(wi_in, 16)
            load_x(1)
            for dst, src in ((wqkv[:, :], w_qkv), (wp[:, :], w_proj),
                             (bias[:, :], b_proj.rearrange("(o d) -> o d", o=1).broadcast_to([P, D]))):
                sp.dma_start(dst, src).then_inc(consts_in, 16)
            load_x(2)
            load_x(3)
            for i, dst in enumerate((QA, QL, QH, KA)):
                sp.dma_start(dst[SHIFT_ROW:P, :, :, :].rearrange("p g h s -> p (g h) s"),
                             fixed_rows[i].rearrange("p (o s) -> p o s", o=1)
                             .broadcast_to([P - SHIFT_ROW, NG * GH, S])).then_inc(fixed_in, 16)
            sp.dma_start(scratch[:, 0, SHIFT_ROW:SHIFT_ROW + SHIFTS, :, :].rearrange("b r h s -> b r (h s)"),
                         zero_rows.rearrange("(o r) n -> o r n", o=1).broadcast_to([B, SHIFTS, H * S])).then_inc(zeros_in, 16)

            def write_parts(b):
                wait_apart(sp, parts_written, b * 96, wi_in, 48)
                wait_apart(sp, lo_ready, b + 1, wi_in, 48)
                row = 0
                for n, names in enumerate(PAIRS):
                    m = len(names)
                    dst_q = scratch[b, 0, row:row + m * DH].rearrange("(a d) h t -> (d h) a t", a=m)
                    dst_k = scratch[b, 1, row:row + m * DH].rearrange("(a d) h t -> (d h) a t", a=m)
                    sp.dma_start(dst_q, at_parity(parts, b)[:, 0, 0:m, :]).then_inc(parts_written, 16)
                    sp.dma_start(dst_k, at_parity(parts, b)[:, 1, n:n + 1, :].broadcast_to([P, m, S])).then_inc(parts_written, 16)
                    row += m * DH

            def load_aug(b, g):
                if not exists(b, g):
                    return
                bb, slot = b + g // NG, g % NG
                first = (slot // 2) * 8 + slot % 2
                wait_apart(sp, e_done, b * (TILES * NG) + TILES * (g - NG + 1), wi_in, 48)
                for side, dst, rows in ((0, QA, ROWS + SHIFTS), (1, KA, ROWS), (0, QL, ROWS), (0, QH, ROWS)):
                    sp.dma_start(dst[0:rows, slot, :, :],
                                 scratch[bb, side, 0:rows, first:first + 7:2, :]).then_inc(aug_in[slot], 16)

            def step(b, g):
                if not isinstance(b, int) or b >= 0:
                    load_aug(b, g + 3)
                if exists(b, g + 1):
                    gn = g + 1
                    wait_apart(sp, mt_copied, b * NG + gn + 1, wi_in, 48)
                    wait_apart(sp, e_done, b * (TILES * NG) + TILES * (gn - NG + 1), wi_in, 48)
                    for part in range(3):
                        sp.dma_start(QA[SHIFT_ROW + part:SHIFT_ROW + part + 1, gn % NG, :, :]
                                     .rearrange("o h (i q) -> o (h i) q", q=P),
                                     mT[16 * part:16 * part + 16, gn % 2, :]).then_inc(shift_in[gn % 2], 16)
                if isinstance(b, int) and b == 0 and g == 0:
                    sp.wait_ge(parts_written, 96 * B)
                if isinstance(b, int) and b == -1 and g == 3:
                    write_parts(B - 1)
                if g == 0 and (not isinstance(b, int) or b >= 2):
                    store(b - 2)

            def store(b):
                wait_apart(sp, f_ready, b + 1, wi_in, 48)
                sp.dma_start(out_v[:, bass.ds(b * TB, TB), :], fo[:, :, :]).then_inc(out_written, 16)

            write_parts(0)
            sp.wait_ge(parts_written, 96)
            sp.wait_ge(fixed_in, 64)
            sp.wait_ge(zeros_in, 16)
            for g in range(3):
                load_aug(0, g)
            with sp.Fori(1, B - 1) as b:
                write_parts(b)
            attention_steps(sp, step)
            store(B - 1)
            wait(sp, out_written, 16 * B)

        @block.gpsimd
        def _(pool):
            nc.gpsimd.memset(Vb[:, :, :, :, :, :], 0.0).then_inc(pool_prep, 1)
            pool.wait_ge(pool_prep, 1)
            nc.gpsimd.memset(msp[:, 3:8, :], 0.0).then_inc(pool_prep, 1)
            for gl in range(2):
                nc.gpsimd.memset(Vb[:, :, :, :, gl, 16 * gl + DH:16 * gl + 2 * DH], 1.0).then_inc(pool_prep, 1)

            def hidden(b):
                for c in range(HC):
                    wait(pool, t1_ready, b * HC + c + 1)
                    wait(pool, up_copied, b * HC + c + 1)
                    if c == 0:
                        wait(pool, down_done, b)
                    nc.gpsimd.tensor_tensor(hT[:, c, :], t1[:, c, :], ups[:, c, :], ALU.mult).then_inc(h_ready, 1)

            def low_parts(b):
                wait(pool, mid_ready, b + 1)
                nc.gpsimd.tensor_tensor(at_parity(parts, b)[:, :, 2, :], rest[:, :, :],
                                        at_parity(parts, b)[:, :, 1, :],
                                        ALU.subtract).then_inc(lo_ready, 1)

            hidden(0)
            hidden(1)
            low_parts(0)
            with pool.Fori(2, B) as b:
                hidden(b)
                low_parts(b - 1)

            def tail():
                low_parts(B - 1)

            def shift_parts(b, g):
                wait_apart(pool, mt_done, b * NG + g, pool_prep, 4)
                wait_apart(pool, red_done, b * (TILES * NG) + TILES * (g + 1), pool_prep, 4)
                flat = rmax[:, g % 2, :, :].rearrange("p h i -> p (h i)")
                for stage in range(4):
                    if stage == 0:
                        ins = nc.gpsimd.tensor_copy(msp[:, 0, :], flat)
                    elif stage == 1:
                        ins = nc.gpsimd.tensor_tensor(rmid[:, :], flat, msp[:, 0, :], ALU.subtract)
                    elif stage == 2:
                        ins = nc.gpsimd.tensor_copy(msp[:, 1, :], rmid[:, :])
                    else:
                        ins = nc.gpsimd.tensor_tensor(msp[:, 2, :], rmid[:, :], msp[:, 1, :], ALU.subtract)
                    if stage < 3:
                        ins.then_inc(shift_chain, 1)
                        wait_apart(pool, shift_chain, b * (3 * NG) + 3 * g + stage + 1, pool_prep, 4)
                    else:
                        ins.then_inc(msp_ready, 1)

            def step(b, g):
                if g % 2 == 0 and exists(b, g):
                    half = g // 2
                    wait(pool, pv_done, b * (4 * NG) + 4 * (g - 2))
                    wait(pool, v_stored, B)
                    wait(pool, pool_prep, 4)
                    for gl in range(2):
                        src = v_all[:, bass.ds(b * TB, TB), :].rearrange(
                            "p t (f c a d) -> p t f c a d", f=2, c=GH, a=2)[:, :, half, :, gl, :]
                        nc.gpsimd.tensor_copy(Vb[:, :, half, :, gl, 16 * gl:16 * gl + DH], src).then_inc(vb_ready, 1)
                for j, after in ((0, 4), (1, 8), (3, 8), (2, 10)):
                    if j == 2 and exists(b, g + 2):
                        shift_parts(b, g + 2)
                    if exists(b, g):
                        wait_apart(pool, exp_done, b * (TILES * NG) + TILES * g + after, pool_prep, 4)
                        blk = PT[:, g % 2, :, KEY_COL[j]:KEY_COL[j] + P]
                        nc.gpsimd.affine_select(out=blk, in_=blk, compare_op=ALU.is_ge, fill=0.0, base=0,
                                                pattern=[[0, GH], [1, P]],
                                                channel_multiplier=-1).then_inc(masked, 1)
                if g == 3 and (not isinstance(b, int) or 1 <= b < B):
                    finish(b - 1)

            def finish(b):
                wait(pool, s_ready, b + 1)
                pool.wait_ge(g_stored, B)
                wait(pool, out_written, b * 16)
                nc.gpsimd.tensor_tensor(sS[:, :, :], sS[:, :, :], gate_all[:, bass.ds(b * TB, TB), :],
                                        ALU.mult).then_inc(sg_ready, 1)
                wait(pool, sg_ready, b + 1)
                nc.gpsimd.tensor_tensor(fo[:, :, :], sS[:, :, :], x_all[:, bass.ds(b * TB, TB), :],
                                        ALU.add).then_inc(f_ready, 1)

            attention_steps(pool, step, tail)

        @block.scalar
        def _(act):
            act.dma_start(idf[:, :], ident_f).then_inc(idf_in, 16)
            for dst, src in ((cosT[:, :], cos_t), (sinT[:, :], sin_t), (idh[:, :], ident_h)):
                act.dma_start(dst, src).then_inc(consts_in, 16)
            def deviation(first, last, count):
                r = rstd[:, first * TB:last * TB]
                act.wait_ge(var_ready, count)
                nc.scalar.activation(r, r, ACT.Sqrt).then_inc(std_ready, 1)

            deviation(0, 2, 1)
            def normalise_in(b, tiles=range(TB)):
                if isinstance(b, int) and b < 3:
                    act.wait_ge(norm_set, b // 2 + 1)
                wait(act, tp_done, b)
                for u in tiles:
                    tile = bass.ds(b * TB + u, 1)
                    last = nc.scalar.activation(xn[:, u, :], x_all[:, b * TB + u, :], ACT.Identity,
                                                bias=offset[:, tile], scale=rstd[:, tile])
                if u == TB - 1:
                    last.then_inc(xn_ready, 1)

            def normed(b):
                wait(act, tp_done, b + 1)
                wait(act, v_done, b)
                nc.scalar.activation(xnT[:, :], bank[0][:, :], ACT.Copy).then_inc(xnT_ready, 1)

            def outer_tanh(b):
                wait(act, down_done, b + 1)
                wait(act, g_stored, b)
                nc.scalar.activation(thf[:, :], bank[1][:, :], ACT.Tanh, scale=0.5).then_inc(thf_ready, 1)

            def chunk(b, c):
                wait(act, gate_done, b * HC + c + 1)
                wait(act, t1_ready, (b - 1) * HC + c + 1)
                nc.scalar.activation(th[:, c, :], bank[2 + 2 * c][:, :], ACT.Tanh, scale=0.5).then_inc(th_ready, 1)
                wait(act, up_done, b * HC + c + 1)
                wait(act, h_ready, (b - 1) * HC + c + 1)
                nc.scalar.activation(ups[:, c, :], bank[3 + 2 * c][:, :], ACT.Copy).then_inc(up_copied, 1)

            def high_parts(b):
                wait(act, roped_ready, b + 1)
                wait(act, parts_written, (b - 1) * 96)
                nc.scalar.activation(at_parity(parts, b)[:, :, 0, :], roped[:, :, :], ACT.Copy).then_inc(hi_ready, 1)

            def mid_parts(b):
                wait(act, rest_ready, b + 1)
                nc.scalar.activation(at_parity(parts, b)[:, :, 1, :], rest[:, :, :], ACT.Copy).then_inc(mid_ready, 1)

            def store_v(b):
                wait(act, v_done, b + 1)
                nc.scalar.activation(v_all[:, bass.ds(b * TB, TB), :].rearrange("p t d -> p (t d)"),
                                     bank[4][:, :], ACT.Copy).then_inc(v_stored, 1)

            def batch(b, first, final=False):
                normed(b)
                if not first:
                    outer_tanh(b - 1)
                chunk(b, 0)
                if not first:
                    high_parts(b - 1)
                chunk(b, 1)
                if not final:
                    normalise_in(b + 1, range(2))
                chunk(b, 2)
                if not final:
                    normalise_in(b + 1, range(2, TB))
                store_v(b)
                if not first:
                    mid_parts(b - 1)

            normalise_in(0)
            batch(0, True)
            deviation(2, B, 2)
            batch(1, False)
            batch(2, False)
            with act.Fori(3, B - 1) as b:
                batch(b, False)
            batch(B - 1, False, True)

            def tail():
                outer_tanh(B - 1)
                high_parts(B - 1)

            def copy_shift(b, g):
                wait(act, mt_done, b * NG + g + 1)
                wait(act, shift_in[g % 2], b * 96 + 48 * ((g - 2) // 2 + 1))
                nc.scalar.activation(mT[:, g % 2, :], bank[X_BANK][0:3 * GH * TB, 0:P // 2].bitcast(bf16),
                                     ACT.Copy).then_inc(mt_copied, 1)

            def copy_o(b, half):
                wait(act, pv_done, b * (4 * NG) + 8 * half + 8)
                wait(act, tr_done, b * 2 + half)
                nc.scalar.activation(OS[:, :], bank[O_BANK][:, :], ACT.Copy).then_inc(o_copied, 1)

            def step(b, g):
                for k in range(TILES):
                    if exists(b, g):
                        n = b * (TILES * NG) + TILES * g + k
                        wait(act, e_done, n + 1)
                        if k == 0:
                            wait(act, pv_done, b * (4 * NG) + 4 * (g - 1))
                        src = bank[ring(g, k)][:, :]
                        if k < 4:
                            dst = PT[:, g % 2, k, 0:512]
                        elif k < 8:
                            dst = PT[:, g % 2, k - 4, 512:1024]
                        else:
                            dst = PT[:, g % 2, 2 * (k - 8):2 * (k - 8) + 2, 1024:1280]
                            src = src.rearrange("p (h q) -> p h q", h=2)
                        nc.scalar.activation(dst, src, ACT.Exp, scale=SCALE).then_inc(exp_done, 1)
                    if k == 2 and exists(b, g + 1):
                        copy_shift(b, g + 1)
                    if k == 7 and g == 2 and (not isinstance(b, int) or b >= 1):
                        wait(act, ant_done, b)
                        wait(act, proj_done, b - 1)
                        nc.scalar.activation(AT[:, :], bank[X_BANK][:, :], ACT.Copy).then_inc(at_copied, 1)
                if isinstance(b, int) and b == -1 and g == 3:
                    mid_parts(B - 1)
                if g == 0 and (not isinstance(b, int) or b >= 1):
                    copy_o(b - 1, 1)
                if g == 2 and exists(b, g) and (not isinstance(b, int) or b >= 0):
                    copy_o(b, 0)

            attention_steps(act, step, tail)

        @block.vector
        def _(dve):
            n = [0]

            def link(ins):
                n[0] += 1
                ins.then_inc(dve_prep, 1)
                dve.wait_ge(dve_prep, n[0])

            def gather(first, last):
                for i in range(first // 2, last // 2):
                    dve.wait_ge(x_in[i], 16)
                    with dve.Fori(2 * i, 2 * i + 2) as b:
                        for u in range(TB):
                            nc.vector.bn_stats(stats[:, b * TB + u, :], x_all[:, b * TB + u, :]).then_inc(dve_prep, 1)
                n[0] += (last - first) * TB

            def statistics(first, last):
                dve.wait_ge(dve_prep, n[0])
                r = slice(first * TB, last * TB)
                me, se, mo, so = (stats[:, r, i] for i in (1, 2, 4, 5))
                nc.vector.tensor_tensor(t6[:, 0, r], me, mo, ALU.add).then_inc(dve_prep, 1)
                nc.vector.tensor_tensor(t6[:, 1, r], me, mo, ALU.subtract).then_inc(dve_prep, 1)
                nc.vector.tensor_tensor(t6[:, 2, r], se, so, ALU.add).then_inc(dve_prep, 1)
                n[0] += 3
                dve.wait_ge(dve_prep, n[0])
                nc.vector.tensor_scalar(mean[:, r], t6[:, 0, r], 0.5, None, ALU.mult).then_inc(dve_prep, 1)
                nc.vector.tensor_tensor(t6[:, 3, r], t6[:, 1, r], t6[:, 1, r], ALU.mult).then_inc(dve_prep, 1)
                nc.vector.tensor_scalar(t6[:, 4, r], t6[:, 2, r], 1.0 / D, EPS, ALU.mult,
                                        ALU.add).then_inc(dve_prep, 1)
                n[0] += 3
                dve.wait_ge(dve_prep, n[0])
                nc.vector.scalar_tensor_tensor(out=rstd[:, r], in0=t6[:, 3, r], scalar=0.25, in1=t6[:, 4, r],
                                               op0=ALU.mult, op1=ALU.add).then_inc(var_ready, 1)

            def invert(first, last, count):
                dve.wait_ge(std_ready, count)
                r = rstd[:, first * TB:last * TB]
                link(nc.vector.reciprocal(r, r))
                nc.vector.scalar_tensor_tensor(out=offset[:, first * TB:last * TB], in0=mean[:, first * TB:last * TB],
                                               scalar=-1.0, in1=r, op0=ALU.mult, op1=ALU.mult).then_inc(norm_set, 1)

            gather(0, 2)
            statistics(0, 2)
            dve.wait_ge(wi_in, 48)
            for w in range(3):
                nc.vector.tensor_scalar(wf[:, w, :, :], wi[:, w, :, :], 1.0 / 127.0, None,
                                        ALU.mult).then_inc(wf_ready, 1)
            invert(0, 2, 1)
            for w, dst in enumerate((wgT, wuT, wdT)):
                dve.wait_ge(wT_done, w + 1)
                nc.vector.tensor_scalar(dst[:, :, :].rearrange("p c k -> p (c k)"), bank[2 + w][:, 0:HID],
                                        0.5 if w == 2 else 1.0, None, ALU.mult).then_inc(wT_ready, 1)

            def outer_gate(b):
                wait(dve, thf_ready, b + 1)
                nc.vector.scalar_tensor_tensor(out=gate_all[:, bass.ds(b * TB, TB), :].rearrange("p t d -> p (t d)"),
                                               in0=thf[:, :], scalar=1.0, in1=bank[1][:, :],
                                               op0=ALU.add, op1=ALU.mult).then_inc(g_stored, 1)

            def gate(b, c):
                wait(dve, th_ready, b * HC + c + 1)
                wait(dve, h_ready, (b - 1) * HC + c + 1)
                nc.vector.scalar_tensor_tensor(out=t1[:, c, :], in0=th[:, c, :], scalar=1.0, in1=bank[2 + 2 * c][:, :],
                                               op0=ALU.add, op1=ALU.mult).then_inc(t1_ready, 1)

            def rest_of(b):
                wait(dve, hi_ready, b + 1)
                wait(dve, lo_ready, b)
                nc.vector.tensor_tensor(rest[:, :, :], roped[:, :, :], at_parity(parts, b)[:, :, 0, :],
                                        ALU.subtract).then_inc(rest_ready, 1)

            def rope(b):
                for i, (done, roped_sem) in enumerate(((q_done, q_roped), (k_done, k_roped))):
                    wait(dve, done, b + 1)
                    if i == 0:
                        wait(dve, roped_ready, b)
                    nc.vector.tensor_tensor(ropc[:, i, :], bank[2 + i][:, :], cosT[:, :],
                                            ALU.mult).then_inc(roped_sem, 1)
                    nc.vector.tensor_tensor(rops[0:64, i, :], bank[2 + i][64:128, :], sinT[64:128, :],
                                            ALU.mult).then_inc(roped_sem, 1)
                    nc.vector.tensor_tensor(rops[64:128, i, :], bank[2 + i][0:64, :], sinT[0:64, :],
                                            ALU.mult).then_inc(roped_sem, 1)
                wait(dve, q_roped, b * 3 + 3)
                wait(dve, k_roped, b * 3 + 3)
                wait(dve, rest_ready, b)
                nc.vector.tensor_tensor(roped[:, :, :], ropc[:, :, :], rops[:, :, :],
                                        ALU.add).then_inc(roped_ready, 1)

            def batch(b):
                outer_gate(b - 1)
                gate(b, 0)
                gate(b, 1)
                rest_of(b - 1)
                gate(b, 2)
                rope(b)

            dve.wait_ge(consts_in, 6 * 16)
            for i in range(2):
                nc.vector.tensor_copy(wqk[:, i, :].rearrange("p (d h) -> p d h", d=DH),
                                      wqkv[:, i * D:(i + 1) * D].rearrange("p (h d) -> p d h", d=DH)
                                      ).then_inc(wf_ready, 1)
            link(nc.vector.tensor_scalar(wp[:, :], wp[:, :], 0.5, None, ALU.mult))
            link(nc.vector.tensor_scalar(bias[:, :], bias[:, :], 0.5, None, ALU.mult))

            for c in range(HC):
                gather(2 * c + 2, 2 * c + 4)
                gate(0, c)
            statistics(2, B)
            rope(0)
            invert(2, B, 2)
            batch(1)
            with dve.Fori(2, B) as b:
                batch(b)

            def tail():
                outer_gate(B - 1)
                rest_of(B - 1)

            def normalise(b, half):
                wait(dve, tr_done, b * 2 + half + 1)
                v = bank[X_BANK][:, :].rearrange("p (t e w) -> p t e w", t=TB, w=2 * DH)
                nc.vector.reciprocal(rl[:, :, :], v[:, :, :, DH]).then_inc(rl_ready, 1)
                wait(dve, rl_ready, b * 2 + half + 1)
                wait(dve, ant_done, b)
                nc.vector.tensor_tensor(AN[:, :, 64 * half:64 * half + 64].rearrange("p t (e d) -> p t e d", d=DH),
                                        v[:, :, :, 0:DH],
                                        rl[:, :, :].rearrange("p t (e o) -> p t e o", o=1).broadcast_to([P, TB, 8, DH]),
                                        ALU.mult).then_inc(norm_ready, 1)

            def projected(b):
                wait(dve, proj_done, b + 1)
                wait(dve, f_ready, b)
                nc.vector.tensor_tensor(sS[:, :, :], bank[X_BANK][:, :].rearrange("p (t d) -> p t d", t=TB),
                                        bias[:, :].rearrange("p (o d) -> p o d", o=1).broadcast_to([P, TB, D]),
                                        ALU.add).then_inc(s_ready, 1)

            def step(b, g):
                later = not isinstance(b, int)
                for k in range(TILES):
                    if exists(b, g + 2):
                        n = b * (TILES * NG) + TILES * (g + 2) + k
                        wait(dve, m_done, n + 1)
                        if k == 0:
                            wait(dve, msp_ready, b * NG + g + 1)
                        src = bank[M_BANK + ring(g + 2, k)]
                        blocks = max_blocks(k)
                        if blocks[0][2] == 1:
                            last = nc.vector.tensor_reduce(rmax[:, g % 2, blocks[0][1]:blocks[0][1] + 2, 1],
                                                           src[:, :].rearrange("p (h q) -> p h q", h=2), AX.X, ALU.max)
                        else:
                            for col, h, i in blocks:
                                last = nc.vector.tensor_reduce(rmax[:, g % 2, h, i:i + 1], src[:, col:col + P * (i + 1)],
                                                               AX.X, ALU.max)
                        last.then_inc(red_done, 1)
                    if k == 8 and g == 1 and (later or b >= 1):
                        normalise(b - 1, 1)
                    if k == 8 and g == 3 and exists(b, g):
                        normalise(b, 0)
                    if k == 9 and g == 2 and (later or b >= 1):
                        projected(b - 1)

            attention_steps(dve, step, tail)
            wait(dve, s_ready, B)
            nc.vector.tensor_tensor(sS[:, :, :], sS[:, :, :], gate_all[:, NT - TB:NT, :], ALU.mult).then_inc(sg_ready, 1)
            dve.wait_ge(sg_ready, B)
            dve.wait_ge(out_written, 16 * (B - 1))
            nc.vector.tensor_tensor(fo[:, :, :], sS[:, :, :], x_all[:, NT - TB:NT, :], ALU.add).then_inc(f_ready, 1)

        @block.tensor
        def _(pe):
            pe.wait_ge(idf_in, 16)
            pe.wait_ge(wf_ready, 3)
            for w in range(3):
                for c in range(HC):
                    last = nc.tensor.transpose(bank[2 + w][:, c * P:(c + 1) * P], wf[:, w, c, :], idf[:, :])
                last.then_inc(wT_done, 1)

            def transpose_in(b):
                wait(pe, xn_ready, b + 1)
                wait(pe, xnT_ready, b)
                for u in range(TB):
                    last = nc.tensor.transpose(bank[0][:, u * P:(u + 1) * P], xn[:, u, :], idf[:, :])
                last.then_inc(tp_done, 1)

            def down(b):
                wait(pe, h_ready, (b + 1) * HC)
                wait(pe, g_stored, b)
                for u in range(TB):
                    for c in range(HC):
                        last = nc.tensor.matmul(bank[1][:, u * P:(u + 1) * P], hT[:, c, u * P:(u + 1) * P],
                                                wdT[:, c, :], start=(c == 0), stop=(c == HC - 1))
                last.then_inc(down_done, 1)

            def products(b):
                wait(pe, xnT_ready, b + 1)
                if isinstance(b, int) and b == 0:
                    pe.wait_ge(wT_ready, 3)
                free_gate = ((q_roped, b * 3), (v_stored, b), (t1_ready, b * HC))
                free_up = ((k_roped, b * 3), (up_copied, (b - 1) * HC + 2), (up_copied, b * HC))
                for c in range(HC):
                    wait(pe, *free_gate[c])
                    nc.tensor.matmul(bank[2 + 2 * c][:, :], wgT[:, c, :], xnT[:, :], start=True,
                                     stop=True).then_inc(gate_done, 1)
                    wait(pe, *free_up[c])
                    nc.tensor.matmul(bank[3 + 2 * c][:, :], wuT[:, c, :], xnT[:, :], start=True,
                                     stop=True).then_inc(up_done, 1)
                if isinstance(b, int) and b == 0:
                    pe.wait_ge(consts_in, 6 * 16)
                    pe.wait_ge(wf_ready, 5)
                wait(pe, t1_ready, b * HC + 1)
                nc.tensor.matmul(bank[2][:, :], wqk[:, 0, :], xnT[:, :], start=True, stop=True).then_inc(q_done, 1)
                wait(pe, up_copied, b * HC + 1)
                nc.tensor.matmul(bank[3][:, :], wqk[:, 1, :], xnT[:, :], start=True, stop=True).then_inc(k_done, 1)
                wait(pe, t1_ready, b * HC + 2)
                for u in range(TB):
                    last = nc.tensor.matmul(bank[4][:, u * P:(u + 1) * P], xnT[:, u * P:(u + 1) * P],
                                            wqkv[:, 2 * D:3 * D], start=True, stop=True)
                last.then_inc(v_done, 1)

            transpose_in(0)
            products(0)
            transpose_in(1)
            down(0)
            products(1)
            with pe.Fori(2, B) as b:
                transpose_in(b)
                down(b - 1)
                products(b)

            down(B - 1)

            def exp_tile(b, g, k):
                wait(pe, exp_done, freed(b, g, k))
                if k == 0:
                    wait(pe, shift_in[g % 2], b * 96 + 48 * (g // 2 + 1))
                    if isinstance(b, int) and b == 0 and g == 0:
                        pe.wait_ge(g_stored, B)
                for col, h, j in exp_blocks(k):
                    last = nc.tensor.matmul(bank[ring(g, k)][:, col:col + S - P * j],
                                            KA[:, g, h, P * j:P * (j + 1)], QA[:, g, h, P * j:S],
                                            start=True, stop=True)
                last.then_inc(e_done, 1)

            def max_tile(b, g, k):
                wait(pe, red_done, freed(b, g, k))
                slot = g % NG
                if k == 0:
                    wait(pe, aug_in[slot], (b + g // NG) * 64 + 64)
                for col, h, i in max_blocks(k):
                    dst, tokens = bank[M_BANK + ring(g, k)], slice(P * i, P * (i + 1))
                    if i > 0:
                        nc.tensor.matmul(dst[:, col:col + P * i], QA[:, slot, h, tokens],
                                         KA[:, slot, h, 0:P * i], start=True, stop=True)
                    for side, start in ((QL, P * i), (QH, P * i + HALF)):
                        last = nc.tensor.matmul(dst[:, col + start:col + start + HALF], side[:, slot, h, tokens],
                                                KA[:, slot, h, start:start + HALF], start=True, stop=True)
                last.then_inc(m_done, 1)

            def values(b, g, piece):
                j = (0, 1, 3, 2)[piece]
                gg = g % NG
                half, gl = gg // 2, gg % 2
                wait(pe, masked, b * (4 * NG) + 4 * g + piece + 1)
                if piece == 0 and gl == 0:
                    halves = b * 2 + g // 2
                    wait(pe, vb_ready, halves * 2 + 2)
                    wait(pe, o_copied, halves)
                for c in range(GH):
                    last = nc.tensor.matmul(bank[O_BANK][32 * c:32 * c + 32, P * j:S], Vb[:, j, half, c, gl, :],
                                            PT[:, gg % 2, c, KEY_COL[j]:KEY_COL[j] + S - P * j],
                                            start=(gl == 0 and piece == 0), stop=(gl == 1 and piece == 3))
                last.then_inc(pv_done, 1)

            def transpose_shift(b, g):
                wait(pe, msp_ready, b * NG + g + 1)
                before = {1: (norm_ready, b * 2 - 1), 2: (mt_copied, b * NG + g), 3: (norm_ready, b * 2),
                          4: (s_ready, b)}[g]
                wait(pe, *before)
                nc.tensor.transpose(bank[X_BANK][:, 0:P // 2].bitcast(bf16),
                                    msp[:, :, :].rearrange("p a m -> p (a m)"), idh[:, :]).then_inc(mt_done, 1)

            def transpose_sums(b, half):
                wait(pe, o_copied, b * 2 + half + 1)
                if exists(b, NG):
                    wait(pe, mt_copied, b * NG + 2 * half + 5)
                elif half == 0:
                    wait(pe, s_ready, b)
                else:
                    wait(pe, norm_ready, b * 2 + 1)
                for u in range(TB):
                    last = nc.tensor.transpose(bank[X_BANK][:, u * P:(u + 1) * P], OS[:, u * P:(u + 1) * P], idf[:, :])
                last.then_inc(tr_done, 1)

            def transpose_back(b):
                wait(pe, norm_ready, b * 2 + 2)
                if exists(b, NG):
                    wait(pe, mt_copied, b * NG + 8)
                for u in range(TB):
                    last = nc.tensor.transpose(bank[X_BANK][:, u * P:(u + 1) * P], AN[:, u, :], idf[:, :])
                last.then_inc(ant_done, 1)

            def project(b):
                wait(pe, at_copied, b + 1)
                for u in range(TB):
                    last = nc.tensor.matmul(bank[X_BANK][:, u * P:(u + 1) * P], AT[:, u * P:(u + 1) * P], wp[:, :],
                                            start=True, stop=True)
                last.then_inc(proj_done, 1)

            def step(b, g):
                later = not isinstance(b, int)
                for k in range(TILES):
                    if exists(b, g):
                        exp_tile(b, g, k)
                    if exists(b, g + 2):
                        max_tile(b, g + 2, k)
                    if k in (1, 5, 7, 9) and exists(b, g - 1):
                        values(b, g - 1, (1, 5, 7, 9).index(k))
                    if k == 2 and exists(b, g + 1):
                        transpose_shift(b, g + 1)
                    if k == 8 and g == 1 and (later or b >= 1):
                        transpose_sums(b - 1, 1)
                    if k == 8 and g == 3 and exists(b, g):
                        transpose_sums(b, 0)
                    if k == 6 and g == 2 and (later or b >= 1):
                        transpose_back(b - 1)
                    if k == 9 and g == 2 and (later or b >= 1):
                        project(b - 1)

            pe.wait_ge(k_roped, 3 * B)
            pe.wait_ge(q_roped, 3 * B)
            pe.wait_ge(v_stored, B)
            pe.wait_ge(t1_ready, HC * B)
            pe.wait_ge(up_copied, HC * B)
            pe.wait_ge(pool_prep, 4)
            attention_steps(pe, step)


def kernel(L0_attn_x, L0_attn_w_qkv, L0_attn_w_proj, L0_attn_b_proj, L0_ffn_w_gate, L0_ffn_w_up, L0_ffn_w_down):
    import numpy as np
    import ml_dtypes
    import concourse.bacc as bacc
    from concourse.bass_utils import run_bass_kernel_spmd as run

    freq = (1.0 / np.float32(10000.0) ** (np.arange(0, DH, 2, dtype=np.float32) / np.float32(DH))).astype(np.float32)
    angle = np.arange(S, dtype=np.float32)[None, :] * np.repeat(np.tile(freq, 2), H)[:, None]
    cos = np.cos(angle).astype(np.float32)
    sin = np.sin(angle).astype(np.float32)
    sin[P // 2:] *= np.float32(-1.0)
    t, pos = np.arange(HALF)[:, None], np.arange(S)[None, :] % P
    fixed = np.zeros((4, P - SHIFT_ROW, S), np.float32)
    at = MASK_ROW - SHIFT_ROW
    fixed[1, at:] = pos < t
    fixed[2, at:] = np.where(pos < HALF, t == 0, pos - HALF < t)
    fixed[3, at:] = np.where(pos % HALF >= t, MASKED, 0.0)
    fixed[3, :SHIFTS] = -1.0
    consts = {
        "cos_t": cos, "sin_t": sin,
        "ident_f": np.eye(P, dtype=np.float32), "ident_h": np.eye(P, dtype=np.float32).astype(ml_dtypes.bfloat16),
        "fixed_rows": fixed.astype(ml_dtypes.bfloat16),
        "zero_rows": np.zeros((SHIFTS, H * S), ml_dtypes.bfloat16),
    }
    arrays = {"x": L0_attn_x, "w_qkv": L0_attn_w_qkv, "w_proj": L0_attn_w_proj, "b_proj": L0_attn_b_proj,
              "w_gate": L0_ffn_w_gate, "w_up": L0_ffn_w_up, "w_down": L0_ffn_w_down, **consts}
    arrays = {f"in_{k}": np.ascontiguousarray(a) for k, a in arrays.items()}
    nc = bacc.Bacc("TRN2", target_bir_lowering=False, num_devices=1)
    args = [nc.dram_tensor(k, a.shape, mybir.dt.from_np(a.dtype), kind="ExternalInput").ap()
            for k, a in arrays.items()]
    scratch = nc.dram_tensor("scratch", (B, 2, ROWS + SHIFTS, H, S), mybir.dt.bfloat16, kind="Internal").ap()
    out = nc.dram_tensor("out_y", (B, S, D), mybir.dt.float32, kind="ExternalOutput").ap()
    attn_ffn_block(nc, *args, scratch, out)
    r = run(nc, [arrays], core_ids=[0])
    return r.results[0]["out_y"]
```
